# Optimizing a Trainium2 kernel written in Bass

```python
import numpy as np
import jax
import jax.numpy as jnp

def _softmax(x, axis=-1):
    return jax.nn.softmax(x, axis=axis)

def _gelu(x):
    return jax.nn.gelu(x, approximate=True)

def _silu(x):
    return jax.nn.silu(x)

def _sigmoid(x):
    return jax.nn.sigmoid(x)

def _layernorm(x, axis=-1, eps=1e-05):
    m = jnp.mean(x, axis=axis, keepdims=True)
    v = jnp.var(x, axis=axis, keepdims=True)
    return (x - m) / jnp.sqrt(v + eps)

def _scatter_add(tgt, idx, src, axis=0):
    return tgt.at[idx].add(src)

def _segment_sum(src, seg, n):
    return jax.ops.segment_sum(src, seg, n)
kernel_name = 'mk_vit_tower_cls_d1_tok_img768_r4_fcd72c'

def setup_inputs(seed: int=0):
    np.random.seed(seed)
    _w = jnp.asarray

    def _rec_inputs():
        import jax
        import jax.numpy as jnp
        _rk = jax.random.key(seed)
        x = 1.64766e-05 + 1.00005 * jax.random.normal(jax.random.fold_in(_rk, 1), (4, 3, 512, 192), jnp.float32)
        cls_tok = 0.02 * jax.random.normal(jax.random.fold_in(_rk, 5), (1, 1, 192), jnp.float32)
        return (x, cls_tok)
    x, cls_tok = _rec_inputs()

    def _L0_tok_setup():
        import jax, jax.numpy as jnp
        import numpy as np
        NUM_BANDS = 6
        D_MODEL = 192
        B, N = (2, 512)
        IN_FEATURES = 3 * NUM_BANDS * 2 * D_MODEL
        key = jax.random.key(seed)
        k_xyz, k_w = jax.random.split(key)
        xyz = jax.random.normal(k_xyz, (B, 3, N, D_MODEL), dtype=jnp.float32)
        freq_bands = 2.0 ** jnp.linspace(0.0, NUM_BANDS - 1, NUM_BANDS).astype(jnp.float32)
        bound = 1.0 / np.sqrt(IN_FEATURES)
        W = jax.random.uniform(k_w, (D_MODEL, IN_FEATURES), dtype=jnp.float32, minval=-bound, maxval=bound)
        return {'xyz': xyz, 'freq_bands': freq_bands, 'W': W}
    _L0_tok_all = _L0_tok_setup()
    _L0_tok_in = {k: v for k, v in _L0_tok_all.items() if k in ('freq_bands', 'W')}
    del _L0_tok_all

    def _L0_attn_setup():
        import jax, jax.numpy as jnp
        import numpy as np
        B, N, D = (4, 2048, 192)
        H, DH = (12, 64)
        INNER = H * DH
        key = jax.random.key(seed)
        k0, k1, k2 = jax.random.split(key, 3)
        return {'x': jax.random.normal(k0, (B, N, D), dtype=jnp.float32), 'w_qkv': jax.random.normal(k1, (D, INNER), dtype=jnp.float32) * 0.02, 'temp': jnp.ones((H, 1), dtype=jnp.float32), 'w_out': jax.random.normal(k2, (INNER, D), dtype=jnp.float32) * 0.02, 'b_out': jnp.zeros((D,), dtype=jnp.float32)}
    _L0_attn_all = _L0_attn_setup()
    _L0_attn_in = {k: v for k, v in _L0_attn_all.items() if k in ('w_qkv', 'temp', 'w_out', 'b_out')}
    del _L0_attn_all

    def _L0_ffn_setup():
        import jax, jax.numpy as jnp
        import numpy as np
        TOP_K = 2
        ROUTED_SCALE = 1.0

        def _swiglu_all(x, gw, uw, dw):
            g = jnp.einsum('th,eih->tei', x, gw)
            u = jnp.einsum('th,eih->tei', x, uw)
            h = jax.nn.silu(g) * u
            return jnp.einsum('tei,ehi->teh', h, dw)
        key = jax.random.key(seed)
        ks = jax.random.split(key, 8)
        B, S, H, I, E, NS = (2, 256, 192, 768, 8, 2)
        w = lambda k, shape: jax.random.normal(k, shape, jnp.float32) * 0.02
        return {'hidden_states': jax.random.normal(ks[0], (B, S, H), jnp.float32), 'gate_w': w(ks[1], (E, H)), 'shared_gate': w(ks[2], (NS, I, H)), 'shared_up': w(ks[3], (NS, I, H)), 'shared_down': w(ks[4], (NS, H, I)), 'routed_gate': w(ks[5], (E, I, H)), 'routed_up': w(ks[6], (E, I, H)), 'routed_down': w(ks[7], (E, H, I))}
    _L0_ffn_all = _L0_ffn_setup()
    _L0_ffn_in = {k: v for k, v in _L0_ffn_all.items() if k in ('gate_w', 'shared_gate', 'shared_up', 'shared_down', 'routed_gate', 'routed_up', 'routed_down')}
    del _L0_ffn_all
    return {'x': x, 'cls_tok': cls_tok, 'L0_tok_freq_bands': _L0_tok_in['freq_bands'], 'L0_tok_W': _L0_tok_in['W'], 'L0_attn_w_qkv': _L0_attn_in['w_qkv'], 'L0_attn_temp': _L0_attn_in['temp'], 'L0_attn_w_out': _L0_attn_in['w_out'], 'L0_attn_b_out': _L0_attn_in['b_out'], 'L0_ffn_gate_w': _L0_ffn_in['gate_w'], 'L0_ffn_shared_gate': _L0_ffn_in['shared_gate'], 'L0_ffn_shared_up': _L0_ffn_in['shared_up'], 'L0_ffn_shared_down': _L0_ffn_in['shared_down'], 'L0_ffn_routed_gate': _L0_ffn_in['routed_gate'], 'L0_ffn_routed_up': _L0_ffn_in['routed_up'], 'L0_ffn_routed_down': _L0_ffn_in['routed_down']}

def reference(x, cls_tok, L0_tok_freq_bands, L0_tok_W, L0_attn_w_qkv, L0_attn_temp, L0_attn_w_out, L0_attn_b_out, L0_ffn_gate_w, L0_ffn_shared_gate, L0_ffn_shared_up, L0_ffn_shared_down, L0_ffn_routed_gate, L0_ffn_routed_up, L0_ffn_routed_down):
    import jax
    import jax.numpy as jnp

    def _L0_tok_ref(xyz, freq_bands, W):
        import jax, jax.numpy as jnp
        import numpy as np
        NUM_BANDS = 6
        D_MODEL = 192
        B, N = (2, 512)
        IN_FEATURES = 3 * NUM_BANDS * 2 * D_MODEL
        b, c, n, d = xyz.shape
        xb = 2.0 * jnp.pi * xyz[..., None] * freq_bands
        feat = jnp.concatenate([jnp.sin(xb), jnp.cos(xb)], axis=-1)
        feat = feat.reshape(b, n, -1)
        return jnp.einsum('bnf,of->bno', feat, W)

    def _L0_attn_ref(x, w_qkv, temp, w_out, b_out):
        import jax, jax.numpy as jnp
        import numpy as np
        B, N, D = (4, 2048, 192)
        H, DH = (12, 64)
        INNER = H * DH
        b, n, _ = x.shape
        h = temp.shape[0]
        w = (x @ w_qkv).reshape(b, n, h, -1).transpose(0, 2, 1, 3)
        norm = jnp.sqrt(jnp.sum(w * w, axis=2, keepdims=True))
        w_normed = w / jnp.maximum(norm, 1e-12)
        logits = jnp.sum(w_normed * w_normed, axis=-1) * temp
        Pi = jax.nn.softmax(logits, axis=-1)
        Pi_norm = Pi / (jnp.sum(Pi, axis=-1, keepdims=True) + 1e-08)
        dots = jnp.einsum('bhn,bhnd->bhd', Pi_norm, w * w)[:, :, None, :]
        attn = 1.0 / (1.0 + dots)
        out = -(w * Pi[..., None]) * attn
        out = out.transpose(0, 2, 1, 3).reshape(b, n, -1)
        return out @ w_out + b_out

    def _L0_ffn_ref(hidden_states, gate_w, shared_gate, shared_up, shared_down, routed_gate, routed_up, routed_down):
        import jax, jax.numpy as jnp
        import numpy as np
        TOP_K = 2
        ROUTED_SCALE = 1.0

        def _swiglu_all(x, gw, uw, dw):
            g = jnp.einsum('th,eih->tei', x, gw)
            u = jnp.einsum('th,eih->tei', x, uw)
            h = jax.nn.silu(g) * u
            return jnp.einsum('tei,ehi->teh', h, dw)
        B, S, H = hidden_states.shape
        T = B * S
        x = hidden_states.reshape(T, H)
        router_logits = x @ gate_w.T
        scores = jax.nn.softmax(router_logits, axis=-1)
        _, topk_idx = jax.lax.top_k(scores, TOP_K)
        topk_w = jnp.take_along_axis(scores, topk_idx, axis=-1)
        topk_w = topk_w / (topk_w.sum(axis=-1, keepdims=True) + 1e-08)
        topk_w = topk_w * ROUTED_SCALE
        E = gate_w.shape[0]
        combine = jnp.zeros((T, E), scores.dtype).at[jnp.arange(T)[:, None], topk_idx].add(topk_w)
        routed_all = _swiglu_all(x, routed_gate, routed_up, routed_down)
        routed_out = jnp.einsum('teh,te->th', routed_all, combine)
        NS = shared_gate.shape[0]
        shared_all = _swiglu_all(x, shared_gate, shared_up, shared_down)
        shared_out = shared_all.sum(axis=1) / NS
        out = (shared_out + routed_out).reshape(B, S, H)
        return out
    h = _L0_tok_ref(x, L0_tok_freq_bands, L0_tok_W)
    h = jnp.concatenate([jnp.broadcast_to(cls_tok, (h.shape[0], 1, h.shape[2])), h], axis=1)
    h = h + _L0_attn_ref(_layernorm(h, axis=-1), L0_attn_w_qkv, L0_attn_temp, L0_attn_w_out, L0_attn_b_out)
    h = h + _L0_ffn_ref(_layernorm(h, axis=-1), L0_ffn_gate_w, L0_ffn_shared_gate, L0_ffn_shared_up, L0_ffn_shared_down, L0_ffn_routed_gate, L0_ffn_routed_up, L0_ffn_routed_down)
    return h

_drawn_inputs = setup_inputs


def setup_inputs(seed=0):
    import zlib

    import numpy as np

    out = dict(_drawn_inputs(seed))
    spreads = {'L0_attn_temp': (1.0, 0.6), 'L0_attn_b_out': (0.0, 0.1)}
    factors = {'cls_tok': 24.788, 'L0_attn_w_qkv': 55.351, 'L0_attn_w_out': 53.588}
    for name, (base, spread) in spreads.items():
        noise = np.random.default_rng([zlib.crc32(name.encode()), seed]).standard_normal(out[name].shape)
        drawn = base * np.exp(spread * noise) if base else spread * noise
        out[name] = jnp.asarray(drawn.astype(out[name].dtype))
    for name, factor in factors.items():
        out[name] = (out[name] * factor).astype(out[name].dtype)
    return out
```

```python
from contextlib import ExitStack, contextmanager

import numpy as np

import concourse.bass as bass
from concourse import mybir

F32 = mybir.dt.float32
I32 = mybir.dt.int32
U32 = mybir.dt.uint32
ALU = mybir.AluOpType
ACT = mybir.ActivationFunctionType
AX_X = mybir.AxisListType.X

B, SEQ, D = 4, 512, 192
P = 128
NX = B * SEQ
NT = NX // P + 1
CLS = NT - 1
T = NX + B
TPB = SEQ // P
KH = D // 2
BANDS = 6
VALS = 3 * D
XB = VALS // P
LEFT = VALS - XB * P
STEPS = XB * BANDS + BANDS // 2
HALF = NX // 2
HT_ = HALF // P
NH, DH = 12, 64
INNER = NH * DH
CH = INNER // P
HPC = P // DH
NE, NS = 8, 2
FF = 768
FC = FF // P
EW = 2 * 2 * FF + FC * D
SLOT_TILES = (2 * T - NE) // P + NE
SLOTS = SLOT_TILES * P
EPS = 1e-5
RING = 3


class Chain:

    def __init__(self, eng, sem):
        self.eng, self.sem, self.count, self.loops = eng, sem, 0, 0

    def __call__(self, ins):
        ins.then_inc(self.sem, 1)
        self.count += 1
        self.eng.wait_ge(self.sem, self.count + self.loops)

    @contextmanager
    def loop(self, trips, links):
        before = self.loops
        with self.eng.Fori(0, trips) as i:
            self.loops = before + i * links
            first = self.count
            yield i
            assert self.count == first + links, (self.count - first, links)
        self.loops = before
        self.count += links * (trips - 1)


def vit_tower(nc, x_t, freqs, w_tok, cls4, w_qkv, temp, w_out, b_out, gate_t, sh_gu, sh_dn, ex_gu, ex_dn,
              c_ident, c_tri, c_heads, c_spread, c_iota, c_valid, out, slots_x, slots_y):
    ctx = ExitStack()
    base = -(-nc.sbuf_base // 32) * 32
    limit = nc.sbuf_base + nc.sbuf_bytes_remaining
    used = {}

    def at(name, shape, offset, dt=F32):
        size = -(-int(np.prod(shape[1:])) * 4 // 32) * 32
        used[name] = nc.alloc_sbuf_tensor_at(name, shape, dt, offset=offset)
        assert offset + size <= limit, (name, offset + size, limit)
        return used[name], offset + size

    with ctx:
        o = base
        h_res, o = at("h_res", [P, NT, D], o)
        xn_t, o = at("xn_t", [KH, 2, T], o)
        ident, o = at("ident", [P, P], o)
        ones, o = at("ones", [P, P], o)
        tri, o = at("tri", [P, P], o)
        stats, o = at("stats", [P, NT, 6], o)
        mean_var, o = at("mean_var", [P, NT, 2], o)
        std, o = at("std", [P, NT], o)
        rstd, o = at("rstd", [P, NT], o)
        gate_sb, o = at("gate_sb", [KH, 2, NE], o)
        iota_sb, o = at("iota_sb", [P, SLOT_TILES + NE], o)
        valid_sb, o = at("valid_sb", [P, NT], o)
        logit, o = at("logit", [P, NT, NE], o)
        score, o = at("score", [P, NT, NE], o)
        top, o = at("top", [P, NT, 8], o)
        top_at, o = at("top_at", [P, NT, 8], o, U32)
        top_f, o = at("top_f", [P, NT, 8], o)
        pick = []
        for j in range(2):
            t_, o = at(f"pick{j}", [P, NT, NE], o)
            pick.append(t_)
        mask, o = at("mask", [P, NT, NE], o)
        place, o = at("place", [P, NT, NE], o)
        total, o = at("total", [P, NT, NE], o)
        row, o = at("row", [P, 4, NT], o)
        weight, o = at("weight", [P, 2, NT], o)
        slot_f, o = at("slot_f", [P, NT], o)
        slot, o = at("slot", [P, 2, NT], o, I32)
        tiles_i, o = at("tiles_i", [P, NE], o, I32)
        tiles_f, o = at("tiles_f", [P, 3, NE], o)
        expert_f, o = at("expert_f", [1, SLOT_TILES], o)
        expert_i, o = at("expert_i", [1, SLOT_TILES], o, I32)
        half_pi, o = at("half_pi", [P, 1], o)
        eps_sb, o = at("eps_sb", [P, 1], o)
        experts_at = o
        rest_at = experts_at + NE * EW * 4

        o = experts_at
        x_sb, o = at("x_sb", [P, XB + 1, NX], o)
        w_tok_sb, o = at("w_tok_sb", [P, STEPS, 2, D], o)
        feat = []
        for r in range(RING):
            t_, o = at(f"feat{r}", [P, 2, HALF], o)
            feat.append(t_)
        turns, o = at("turns", [P, HALF], o, I32)
        phase = []
        for r in range(RING):
            t_, o = at(f"phase{r}", [P, 2, HALF], o)
            phase.append(t_)
        freq_sb, o = at("freq_sb", [P, BANDS + BANDS // 2], o)
        w_qkv_sb, o = at("w_qkv_sb", [KH, 2, INNER], o)
        w_out_sb, o = at("w_out_sb", [P, CH, D], o)
        heads_sb, o = at("heads_sb", [P, CH, NH], o)
        spread_sb, o = at("spread_sb", [NH, CH, P], o)
        temp_sb, o = at("temp_sb", [NH, 1], o)
        bias_sb, o = at("bias_sb", [P, D], o)
        assert o <= limit - NT * D * 4
        o = experts_at
        w_sb, o = at("w_sb", [P, CH, SEQ + 1], o)
        w_sq, o = at("w_sq", [P, CH, SEQ + 1], o)
        wp, o = at("wp", [P, CH, SEQ + 1], o)
        scratch, o = at("scratch", [P, SEQ], o)
        w_out_b, o = at("w_out_b", [P, CH, D], o)
        norm_sq, o = at("norm_sq", [P, CH], o)
        inv_sq, o = at("inv_sq", [P, CH], o)
        norm_lhs, o = at("norm_lhs", [P, CH, NH], o)
        lg, o = at("lg", [NH, SEQ + 1], o)
        pi, o = at("pi", [NH, SEQ + 2], o)
        soft, o = at("soft", [NH, 4], o)
        dots, o = at("dots", [P, CH], o)
        cls_dots, o = at("cls_dots", [P, CH], o)
        neg_attn, o = at("neg_attn", [P, CH], o)
        wp_cls, o = at("wp_cls", [P, CH, B], o)

        ex_gu_sb = nc.alloc_sbuf_tensor_at("ex_gu_sb", [KH, NE, 2, 2 * FF], F32, offset=experts_at)
        ex_dn_sb, o = at("ex_dn_sb", [P, NE, FC, D], experts_at + NE * 2 * 2 * FF * 4)
        assert o == rest_at
        xn_at = (limit - NT * D * 4) // 32 * 32
        xn, _ = at("xn", [P, NT, D], xn_at)
        zeros, _ = at("zeros", [P, 4, D], xn_at)
        sh_at = rest_at
        sh_gu_sb = [nc.alloc_sbuf_tensor_at("sh_gu0", [KH, 2, 2 * FF], F32, offset=sh_at), None]
        sh_dn0, o = at("sh_dn0", [P, FC, D], sh_at + 2 * 2 * FF * 4)
        before, _ = at("before", [1, SLOT_TILES, NE], o)
        sh_silu, o = at("sh_silu", [P, 2, SEQ], o)
        sh_h, o = at("sh_h", [P, 2, SEQ], o)
        assert o <= xn_at
        o = rest_at
        sh_gu_sb[1], o = at("sh_gu1", [KH, 2, 2 * FF], o)
        sh_dn1, o = at("sh_dn1", [P, FC, D], o)
        sh_dn_sb = [sh_dn0, sh_dn1]
        sx, o = at("sx", [P, 2, D], o)
        sx_t = [None, None]
        sx_t[0], o = at("sx_t0", [KH, 2, P], o)
        sx_t[1], o = at("sx_t1", [KH, 2, P], o)
        hid, o = at("hid", [P, 2, FF], o)
        hid_t = [None, None]
        hid_t[0], o = at("hid_t0", [P, FC, P], o)
        hid_t[1], o = at("hid_t1", [P, FC, P], o)
        sy, o = at("sy", [P, 2, D], o)
        o = experts_at
        sh_silu1, o = at("sh_silu1", [P, 2, SEQ], o)
        sh_h1, o = at("sh_h1", [P, 2, SEQ], o)
        gat, o = at("gat", [P, 2, NT, D], o)

        ps = ctx.enter_context(nc.psum_tensor("ps", [P, 8, 512], F32))

        def sem(name):
            return ctx.enter_context(nc.semaphore(name))

        s_const = sem("constants_loaded")
        s_x = [sem(f"x_half{i}_loaded") for i in range(2)]
        s_wtok = sem("w_tok_loaded")
        s_attnw = sem("attention_weights_loaded")
        s_zero = sem("zeros_ready")
        s_own = sem("vector_constants_ready")
        s_zeroed = sem("slots_zeroed")
        s_turns = sem("phases_ready")
        s_feat = sem("features_ready")
        s_used = sem("features_used")
        s_hrow = sem("token_rows_evacuated")
        s_dchain = sem("vector_chain")
        s_achain = sem("scalar_chain")
        s_var = sem("variances_ready")
        s_std = sem("deviations_ready")
        s_xn = sem("normalised_ready")
        s_xnp = sem("normalised_transposed")
        s_xnt = sem("normalised_columns_ready")
        s_hb = sem("bias_added")
        s_q = sem("projection_ready")
        s_qe = sem("projection_evacuated")
        s_nl = sem("norm_weights_ready")
        s_lg = sem("logits_ready")
        s_mx = sem("logit_maximum_ready")
        s_exp = sem("attention_exp_ready")
        s_pi = sem("pi_ready")
        s_pb = sem("pi_spread")
        s_pbe = sem("pi_spread_used")
        s_wo = sem("scaled_w_out_ready")
        s_y = sem("attention_out_ready")
        s_ye = sem("attention_out_added")
        s_rl = sem("router_logits_ready")
        s_rm = sem("router_maximum_taken")
        s_re = sem("router_exp_ready")
        s_mask = sem("mask_ready")
        s_cnt = sem("counts_ready")
        s_slot = sem("slots_ready")
        s_te = sem("tile_experts_ready")
        s_scat = sem("rows_scattered")
        s_shw = [sem(f"shared{i}_weights_loaded") for i in range(2)]
        s_exw = sem("expert_weights_loaded")
        s_gu = sem("shared_gate_up_ready")
        s_silu = sem("shared_silu_ready")
        s_h = sem("shared_hidden_ready")
        s_dn = sem("shared_hidden_used")
        s_ya = sem("shared_out_added")
        s_sx = sem("slot_rows_loaded")
        s_sxe = [sem(f"slot_rows_loaded{i}") for i in range(2)]
        s_xt = sem("slot_rows_transposed")
        s_xte = sem("slot_columns_ready")
        s_rg = sem("routed_gate_up_ready")
        s_rs = sem("routed_silu_ready")
        s_rh = sem("routed_hidden_ready")
        s_ht = sem("routed_hidden_transposed")
        s_hte = sem("routed_hidden_columns_ready")
        s_ry = sem("routed_out_ready")
        s_rye = sem("routed_out_evacuated")
        s_rst = [sem(f"routed_out_stored{i}") for i in range(2)]
        s_gat = sem("rows_gathered")
        s_fin = sem("rows_final")
        s_out = sem("out_stored")

        block = ctx.enter_context(nc.Block())

        def tile_rows(t):
            return P if t < CLS else B

        def columns(t):
            return slice(t * P, t * P + tile_rows(t))

        SHB = NS * 0 + FC

        @block.sync
        def _(sp):
            sp.dma_start(freq_sb[:], freqs).then_inc(s_const, 16)
            for half in range(2):
                cols = slice(half * HALF, half * HALF + HALF)
                sp.dma_start(x_sb[:, 0:XB, cols], x_t[0:XB * P, cols].rearrange("(c p) n -> p c n", p=P)).then_inc(s_x[half], 16)
                for part in range(P // LEFT):
                    sp.dma_start(x_sb[part * LEFT:(part + 1) * LEFT, XB, cols], x_t[XB * P:, cols]).then_inc(s_x[half], 16)
            sp.dma_start(ident[:], c_ident).then_inc(s_const, 16)
            sp.dma_start(h_res[0:B, CLS, :], cls4).then_inc(s_const, 16)
            sp.dma_start(tri[:], c_tri).then_inc(s_const, 16)
            sp.dma_start(gate_sb[:], gate_t).then_inc(s_const, 16)
            sp.dma_start(iota_sb[:], c_iota).then_inc(s_const, 16)
            sp.dma_start(valid_sb[:], c_valid).then_inc(s_const, 16)
            sp.dma_start(w_qkv_sb[:], w_qkv).then_inc(s_attnw, 16)
            sp.dma_start(w_out_sb[:], w_out).then_inc(s_attnw, 16)
            sp.dma_start(heads_sb[:], c_heads).then_inc(s_attnw, 16)
            sp.dma_start(spread_sb[:], c_spread).then_inc(s_attnw, 16)
            sp.dma_start(temp_sb[:], temp).then_inc(s_attnw, 16)
            sp.dma_start(bias_sb[:], b_out).then_inc(s_attnw, 16)
            sp.wait_ge(s_zero, 1)
            zero_rows = slots_x.rearrange("(n a p) d -> n p a d", p=P, a=4)
            for n in range(SLOT_TILES // 4):
                sp.dma_start(zero_rows[n], zeros[:]).then_inc(s_zeroed, 16)
            sp.wait_ge(s_ye, B + 1)
            sp.dma_start(sh_gu_sb[0][:], sh_gu[0]).then_inc(s_shw[0], 16)
            sp.dma_start(sh_dn_sb[0][:], sh_dn[0]).then_inc(s_shw[0], 16)
            for e in range(NE):
                sp.dma_start(ex_gu_sb[:, e], ex_gu[e]).then_inc(s_exw, 16)
                sp.dma_start(ex_dn_sb[:, e], ex_dn[e]).then_inc(s_exw, 16)
            sp.wait_ge(s_scat, 16 * 2 * NT)
            sp.wait_ge(s_ya, B + 1)
            for n in range(2):
                sp.dma_start(sx[:, n], slots_x[n * P:(n + 1) * P, :]).then_inc(s_sxe[n], 16)
            sp.dma_start(sh_gu_sb[1][:], sh_gu[1]).then_inc(s_shw[1], 16)
            sp.dma_start(sh_dn_sb[1][:], sh_dn[1]).then_inc(s_shw[1], 16)
            with sp.Fori(0, SLOT_TILES // 2 - 1) as i:
                for n in range(2):
                    sp.wait_ge(s_xt, 2 * i + n + 1)
                    sp.dma_start(sx[:, n], slots_x[bass.ds((2 * i + 2 + n) * P, P), :]).then_inc(s_sxe[n], 16)
            for b in range(B):
                sp.wait_ge(s_fin, (b + 1) * TPB)
                sp.dma_start(out[b, 1:, :].rearrange("(t p) d -> p t d", p=P), h_res[:, b * TPB:(b + 1) * TPB, :]).then_inc(s_out, 16)
            sp.wait_ge(s_fin, CLS + 1)
            sp.dma_start(out[:, 0, :], h_res[0:B, CLS, :]).then_inc(s_out, 16)
            sp.wait_ge(s_out, 16 * (B + 1))

        @block.gpsimd
        def _(pool):
            nc.gpsimd.memset(zeros[:], 0.0).then_inc(s_zero, 1)
            pool.wait_ge(s_attnw, 16 * 6)
            pool.wait_ge(s_xn, NT)
            for t in range(NT):
                r = tile_rows(t)
                last = nc.gpsimd.tensor_tensor(h_res[0:r, t], h_res[0:r, t], bias_sb[0:r, :], ALU.add)
                last.then_inc(s_hb, 1)
            pool.wait_ge(s_slot, 2)
            pool.wait_ge(s_zeroed, 16 * (SLOT_TILES // 4))
            for t in range(NT):
                r = tile_rows(t)
                for j in range(2):
                    nc.gpsimd.indirect_dma_start(
                        slots_x, bass.IndirectOffsetOnAxis(ap=slot[0:r, j, t:t + 1], axis=0),
                        xn[0:r, t, :], None).then_inc(s_scat, 16)
            for n in range(2):
                pool.wait_ge(s_rst[n], 16 * (SLOT_TILES // 2))
            pool.wait_ge(s_ry, SLOT_TILES)
            for t in range(NT):
                r = tile_rows(t)
                for j in range(2):
                    nc.gpsimd.indirect_dma_start(
                        gat[0:r, j, t, :], None, slots_y,
                        bass.IndirectOffsetOnAxis(ap=slot[0:r, j, t:t + 1], axis=0)).then_inc(s_gat, 16)

        @block.scalar
        def _(act):
            act.dma_start(w_tok_sb[:], w_tok).then_inc(s_wtok, 16)
            act.wait_ge(s_own, 1)

            def sines(step, r):
                act.wait_ge(s_turns, 2 * step + 2)
                act.wait_ge(s_used, step + 1)
                nc.scalar.activation(feat[r][:, 0], phase[r][:, 0], ACT.Sin, scale=6.283185).then_inc(s_feat, 1)
                nc.scalar.activation(feat[r][:, 1], phase[r][:, 1], ACT.Sin, bias=half_pi[:], scale=-6.283185).then_inc(s_feat, 1)

            with act.Fori(0, 2) as half:
                with act.Fori(0, XB) as c:
                    for k in range(BANDS):
                        sines(half * STEPS + c * BANDS + k, k % RING)
                for k in range(BANDS // 2):
                    sines(half * STEPS + XB * BANDS + k, k % RING)
                act.wait_ge(s_used, half * STEPS + STEPS + RING)
                for j in range(HT_):
                    nc.scalar.copy(h_res[:, bass.ds(half * HT_ + j, 1), :], ps[:, j:j + 1, 0:D]).then_inc(s_hrow, 1)

            def norm_columns(n):
                act.wait_ge(s_var, n + 1)
                nc.scalar.activation(std[:], mean_var[:, :, 1], ACT.Sqrt, bias=eps_sb[:]).then_inc(s_std, 1)
                for t in range(NT):
                    r = tile_rows(t)
                    act.wait_ge(s_xnp, n * NT + t + 1)
                    nc.scalar.copy(xn_t[:, :, columns(t)], ps[0:KH, t % 4, 0:2 * r].rearrange("p (k n) -> p k n", k=2)).then_inc(s_xnt, 1)

            norm_columns(0)
            with act.Fori(0, B) as b:
                for c in range(CH):
                    act.wait_ge(s_q, b * (CH + 1) + c + 1)
                    nc.scalar.copy(w_sb[:, c, 0:SEQ], ps[:, c % 2, :])
                    nc.scalar.activation(w_sq[:, c, 0:SEQ], ps[:, c % 2, :], ACT.Square,
                                         accum_out=norm_sq[:, c:c + 1]).then_inc(s_qe, 1)
                act.wait_ge(s_q, b * (CH + 1) + CH + 1)
                nc.scalar.copy(w_sb[:, :, SEQ], ps[:, 2, 0:CH])
                nc.scalar.activation(w_sq[:, :, SEQ], ps[:, 2, 0:CH], ACT.Square).then_inc(s_qe, 1)
                act.wait_ge(s_mx, b + 1)
                nc.scalar.activation(pi[:, 0:SEQ + 1], lg[:], ACT.Exp, bias=soft[:, 0:1],
                                     accum_out=soft[:, 1:2]).then_inc(s_exp, 1)
            norm_columns(1)
            act.wait_ge(s_rm, 1)
            nc.scalar.activation(score[:], logit[:], ACT.Exp).then_inc(s_re, 1)

            def shared(s, silu):
                def block_(first, n):
                    for c in range(FC):
                        act.wait_ge(s_gu, first + c + 1)
                        nc.scalar.activation(silu[:, c % 2, 0:n], ps[:, 2 * (c % 2), 0:n], ACT.Silu).then_inc(s_silu, 1)
                with act.Fori(0, B) as b:
                    block_((s * (B + 1) + b) * FC, SEQ)
                block_((s * (B + 1) + B) * FC, B)

            shared(0, sh_silu)
            act.wait_ge(s_ya, B + 1)
            with act.Fori(0, SLOT_TILES // 2) as i:
                for n in range(2):
                    act.wait_ge(s_rg, 2 * i + n + 1)
                    nc.scalar.activation(hid[:, n, :], ps[:, 3 * n:3 * n + 2, :].rearrange("p a n -> p (a n)")[:, 0:FF], ACT.Silu).then_inc(s_rs, 1)
                    act.wait_ge(s_ht, 2 * i + n + 1)
                    nc.scalar.copy(hid_t[n][:], ps[:, 6:8, :].rearrange("p a n -> p (a n)")[:, 0:FF].rearrange("p (c n) -> p c n", c=FC)).then_inc(s_hte, 1)
                    act.wait_ge(s_rye, 2 * i + n + 1)
                    act.dma_start(slots_y[bass.ds((2 * i + n) * P, P), :], sy[:, n]).then_inc(s_rst[n], 16)
            act.wait_ge(s_ry, SLOT_TILES)
            shared(1, sh_silu1)

        @block.vector
        def _(dve):
            link = Chain(dve, s_dchain)
            nc.vector.memset(half_pi[:], float(np.pi / 2))
            nc.vector.memset(eps_sb[:], EPS)
            nc.vector.memset(ones[:], 1.0).then_inc(s_used, RING)
            nc.vector.memset(std[:], 1.0).then_inc(s_feat, 2 * RING)
            nc.vector.memset(mean_var[:], 1.0).then_inc(s_own, 1)
            dve.wait_ge(s_own, 1)

            def phases(step, r, x, f):
                link(nc.vector.tensor_scalar(turns[:], x, freq_sb[:, f:f + 1], None, ALU.mult))
                dve.wait_ge(s_feat, 2 * step + 2)
                nc.vector.scalar_tensor_tensor(out=phase[r][:, 0], in0=x, scalar=freq_sb[:, f:f + 1], in1=turns[:],
                                               op0=ALU.mult, op1=ALU.subtract).then_inc(s_turns, 1)
                dve.wait_ge(s_turns, 2 * step + 1)
                nc.vector.tensor_scalar(phase[r][:, 1].bitcast(I32), phase[r][:, 0].bitcast(I32), 0x7FFFFFFF, None,
                                        ALU.bitwise_and).then_inc(s_turns, 1)

            dve.wait_ge(s_const, 16 * 7)
            dve.wait_ge(s_x[0], 48)
            dve.wait_ge(s_x[1], 48)
            with link.loop(2, STEPS) as half:
                with link.loop(XB, BANDS) as c:
                    for k in range(BANDS):
                        phases(half * STEPS + c * BANDS + k, k % RING,
                               x_sb[:, bass.ds(c, 1), bass.ds(half * HALF, HALF)].rearrange("p a n -> p (a n)"), k)
                for k in range(BANDS // 2):
                    phases(half * STEPS + XB * BANDS + k, k % RING, x_sb[:, XB, bass.ds(half * HALF, HALF)], BANDS + k)

            def normalise(n):
                for t in range(NT):
                    r = tile_rows(t)
                    last = nc.vector.bn_stats(stats[0:r, t], h_res[0:r, t, :])
                link(last)
                for t in range(NT):
                    r = tile_rows(t)
                    last = nc.vector.bn_aggr(mean_var[0:r, t], stats[0:r, t])
                last.then_inc(s_var, 1)
                dve.wait_ge(s_std, n + 1)
                link(nc.vector.reciprocal(rstd[:], std[:]))
                for t in range(NT):
                    r = tile_rows(t)
                    nc.vector.tensor_scalar(xn[0:r, t], h_res[0:r, t, :], mean_var[0:r, t, 0:1], rstd[0:r, t:t + 1],
                                            ALU.subtract, ALU.mult).then_inc(s_xn, 1)

            dve.wait_ge(s_hrow, CLS)
            dve.wait_ge(s_zeroed, 16 * (SLOT_TILES // 4))
            normalise(0)
            dve.wait_ge(s_attnw, 16 * 6)
            with link.loop(B, 19) as b:
                dve.wait_ge(s_qe, b * (CH + 1) + CH + 1)
                link(nc.vector.tensor_tensor(norm_sq[:], norm_sq[:], w_sq[:, :, SEQ], ALU.add))
                link(nc.vector.tensor_scalar(norm_sq[:], norm_sq[:], 1e-24, None, ALU.max))
                link(nc.vector.reciprocal(inv_sq[:], norm_sq[:]))
                nc.vector.tensor_tensor(norm_lhs[:], heads_sb[:], inv_sq[:].rearrange("p (c a) -> p c a", a=1).to_broadcast([P, CH, NH]), ALU.mult).then_inc(s_nl, 1)
                dve.wait_ge(s_lg, b + 1)
                nc.vector.tensor_scalar(lg[:, 0:SEQ], ps[0:NH, 3, :], temp_sb[:], None, ALU.mult)
                link(nc.vector.tensor_scalar(lg[:, SEQ:SEQ + 1], ps[0:NH, 2, 32:33], temp_sb[:], None, ALU.mult))
                nc.vector.tensor_reduce(soft[:, 0:1], lg[:], AX_X, ALU.max, negate=True).then_inc(s_mx, 1)
                dve.wait_ge(s_exp, b + 1)
                link(nc.vector.reciprocal(soft[:, 2:3], soft[:, 1:2]))
                link(nc.vector.tensor_scalar(pi[:, 0:SEQ + 1], pi[:, 0:SEQ + 1], soft[:, 2:3], None, ALU.mult))
                link(nc.vector.tensor_reduce(soft[:, 3:4], pi[:, 0:SEQ + 1], AX_X, ALU.add))
                link(nc.vector.tensor_scalar(soft[:, 3:4], soft[:, 3:4], 1e-8, None, ALU.add))
                nc.vector.reciprocal(pi[:, SEQ + 1:SEQ + 2], soft[:, 3:4]).then_inc(s_pi, 1)
                for c in range(CH):
                    dve.wait_ge(s_pb, b * CH + c + 1)
                    link(nc.vector.tensor_tensor(wp[:, c, 0:SEQ], ps[:, c % 2, :], w_sb[:, c, 0:SEQ], ALU.mult))
                    nc.vector.scalar_tensor_tensor(out=scratch[:], in0=wp[:, c, 0:SEQ], scalar=1.0, in1=w_sb[:, c, 0:SEQ],
                                                   op0=ALU.mult, op1=ALU.mult, accum_out=dots[:, c:c + 1]).then_inc(s_pbe, 1)
                spread = ps[:, 2, 64:64 + 2 * CH].rearrange("p (c a) -> p c a", a=2)
                link(nc.vector.tensor_tensor(wp[:, :, SEQ], spread[:, :, 0], w_sb[:, :, SEQ], ALU.mult))
                link(nc.vector.tensor_tensor(cls_dots[:], wp[:, :, SEQ], w_sb[:, :, SEQ], ALU.mult))
                dve.wait_ge(s_pbe, b * CH + CH)
                link(nc.vector.tensor_tensor(dots[:], dots[:], cls_dots[:], ALU.add))
                link(nc.vector.tensor_tensor(dots[:], dots[:], spread[:, :, 1], ALU.mult))
                link(nc.vector.tensor_scalar(dots[:], dots[:], 1.0, -1.0, ALU.add, ALU.mult))
                nc.vector.reciprocal(neg_attn[:], dots[:]).then_inc(s_wo, 1)
                dve.wait_ge(s_wo, 2 * b + 1)
                nc.vector.tensor_tensor(wp_cls[:, :, bass.ds(b, 1)].rearrange("p c a -> p (c a)"), wp[:, :, SEQ], neg_attn[:], ALU.mult)
                nc.vector.tensor_tensor(w_out_b[:], w_out_sb[:], neg_attn[:].rearrange("p (c a) -> p c a", a=1).to_broadcast([P, CH, D]), ALU.mult).then_inc(s_wo, 1)
                dve.wait_ge(s_y, b + 1)
                dve.wait_ge(s_hb, NT)
                for t in range(TPB):
                    last = nc.vector.tensor_tensor(h_res[:, bass.ds(b * TPB + t, 1), :], ps[:, 4 + t:5 + t, 0:D],
                                                   h_res[:, bass.ds(b * TPB + t, 1), :], ALU.add)
                last.then_inc(s_ye, 1)
            dve.wait_ge(s_y, B + 1)
            nc.vector.tensor_tensor(h_res[0:B, CLS, :], ps[0:B, 0, 0:D], h_res[0:B, CLS, :], ALU.add).then_inc(s_ye, 1)
            dve.wait_ge(s_ye, B + 1)
            normalise(1)

            dve.wait_ge(s_rl, 1)
            lg_ps = ps[:, 4, 0:NT * NE].rearrange("p (t e) -> p t e", e=NE)
            link(nc.vector.tensor_reduce(row[:, 0], lg_ps, AX_X, ALU.max))
            nc.vector.tensor_tensor(logit[:], lg_ps, row[:, 0].rearrange("p (t a) -> p t a", a=1).to_broadcast([P, NT, NE]),
                                    ALU.subtract).then_inc(s_rm, 1)
            dve.wait_ge(s_re, 1)
            link(nc.vector.tensor_reduce(row[:, 1], score[:], AX_X, ALU.add))
            link(nc.vector.reciprocal(row[:, 2], row[:, 1]))
            link(nc.vector.tensor_tensor(score[:], score[:], row[:, 2].rearrange("p (t a) -> p t a", a=1).to_broadcast([P, NT, NE]), ALU.mult))
            for t in range(NT):
                last = nc.vector.max(top[:, t], score[:, t])
            link(last)
            for t in range(NT):
                last = nc.vector.max_index(top_at[:, t], top[:, t], score[:, t])
            link(last)
            link(nc.vector.tensor_copy(top_f[:], top_at[:]))
            experts_row = iota_sb[:, SLOT_TILES:].rearrange("p (a e) -> p a e", a=1).to_broadcast([P, NT, NE])
            real = valid_sb[:].rearrange("p (t a) -> p t a", a=1).to_broadcast([P, NT, NE])
            for j in range(2):
                link(nc.vector.tensor_tensor(pick[j][:], experts_row, top_f[:, :, j:j + 1].to_broadcast([P, NT, NE]), ALU.is_equal))
                link(nc.vector.tensor_tensor(pick[j][:], pick[j][:], real, ALU.mult))
            nc.vector.tensor_tensor(mask[:], pick[0][:], pick[1][:], ALU.add).then_inc(s_mask, 1)
            link(nc.vector.tensor_tensor(row[:, 3], top[:, :, 0], top[:, :, 1], ALU.add))
            link(nc.vector.tensor_scalar(row[:, 3], row[:, 3], 1e-8, None, ALU.add))
            link(nc.vector.reciprocal(row[:, 0], row[:, 3]))
            for j in range(2):
                nc.vector.tensor_tensor(weight[:, j], top[:, :, j], row[:, 0], ALU.mult)
            dve.wait_ge(s_cnt, 1)
            in_tile = ps[:, 4, 0:NT * NE].rearrange("p (t e) -> p t e", e=NE)
            of_tile = ps[:, 5, 0:NT * NE].rearrange("p (t e) -> p t e", e=NE)
            link(nc.vector.tensor_copy(place[:], of_tile))
            for e in range(NE):
                last = nc.vector.tensor_tensor_scan(total[:, :, e], ones[:, 0:NT], place[:, :, e], 0.0, ALU.mult, ALU.add)
            link(last)
            link(nc.vector.tensor_scalar(tiles_i[:], total[:, CLS], 1.0 / P, 0.5 - 0.5 / P, ALU.mult, ALU.add))
            link(nc.vector.tensor_copy(tiles_f[:, 0], tiles_i[:]))
            link(nc.vector.tensor_tensor_scan(tiles_f[:, 1], ones[:, 0:NE], tiles_f[:, 0], 0.0, ALU.mult, ALU.add))
            link(nc.vector.tensor_tensor(tiles_f[:, 2], tiles_f[:, 1], tiles_f[:, 0], ALU.subtract))
            link(nc.vector.tensor_scalar(tiles_f[:, 2], tiles_f[:, 2], float(P), None, ALU.mult))
            link(nc.vector.tensor_tensor(place[:], total[:], place[:], ALU.subtract))
            link(nc.vector.tensor_tensor(place[:], place[:], in_tile, ALU.add))
            link(nc.vector.tensor_tensor(place[:], place[:], tiles_f[:, 2:3].to_broadcast([P, NT, NE]), ALU.add))
            for j in range(2):
                link(nc.vector.tensor_tensor(pick[j][:], pick[j][:], place[:], ALU.mult))
                link(nc.vector.tensor_reduce(slot_f[:], pick[j][:], AX_X, ALU.add))
                nc.vector.tensor_copy(slot[:, j], slot_f[:]).then_inc(s_slot, 1)
                dve.wait_ge(s_slot, j + 1)
            link(nc.vector.tensor_tensor(before[:], tiles_f[0:1, 1:2].to_broadcast([1, SLOT_TILES, NE]),
                                         iota_sb[0:1, 0:SLOT_TILES].rearrange("p (t a) -> p t a", a=1).to_broadcast([1, SLOT_TILES, NE]), ALU.is_le))
            link(nc.vector.tensor_reduce(expert_f[:], before[:], AX_X, ALU.add))
            nc.vector.tensor_scalar(expert_i[:], expert_f[:], float(NE - 1), None, ALU.min).then_inc(s_te, 1)

            def shared(s, silu, hidden):
                def block_(nth, n):
                    for c in range(FC):
                        dve.wait_ge(s_silu, nth * FC + c + 1)
                        dve.wait_ge(s_dn, nth * FC + c + 1)
                        nc.vector.tensor_tensor(hidden[:, c % 2, 0:n], silu[:, c % 2, 0:n], ps[:, 2 * (c % 2) + 1, 0:n],
                                                ALU.mult).then_inc(s_h, 1)
                    dve.wait_ge(s_dn, nth * FC + FC + 2)
                first = s * (B + 1)
                with dve.Fori(0, B) as b:
                    block_(first + b, SEQ)
                    for t in range(TPB):
                        last = nc.vector.scalar_tensor_tensor(
                            out=h_res[:, bass.ds(b * TPB + t, 1), :], in0=ps[:, 4 + t:5 + t, 0:D], scalar=1.0 / NS,
                            in1=h_res[:, bass.ds(b * TPB + t, 1), :], op0=ALU.mult, op1=ALU.add)
                    last.then_inc(s_ya, 1)
                block_(first + B, B)
                nc.vector.scalar_tensor_tensor(out=h_res[0:B, CLS, :], in0=ps[0:B, 4, 0:D], scalar=1.0 / NS,
                                               in1=h_res[0:B, CLS, :], op0=ALU.mult, op1=ALU.add).then_inc(s_ya, 1)

            nc.vector.memset(row[:, 0, 0:1], 0.0).then_inc(s_dn, 2)
            shared(0, sh_silu, sh_h)
            dve.wait_ge(s_ya, B + 1)
            dve.wait_ge(s_scat, 16 * 2 * NT)

            def slot_columns(j, n):
                dve.wait_ge(s_xt, j + 1)
                nc.vector.tensor_copy(sx_t[n][:], ps[0:KH, 3 * n, 0:2 * P].rearrange("p (k n) -> p k n", k=2)).then_inc(s_xte, 1)

            def routed(j, n, more):
                dve.wait_ge(s_rs, j + 1)
                up = ps[:, 3 * n:3 * n + 3, :].rearrange("p a n -> p (a n)")[:, FF:2 * FF]
                nc.vector.tensor_tensor(hid[:, n], hid[:, n], up, ALU.mult).then_inc(s_rh, 1)
                if more:
                    slot_columns(j + 2, n)
                dve.wait_ge(s_ry, j + 1)
                nc.vector.tensor_copy(sy[:, n], ps[:, 7, 256:256 + D]).then_inc(s_rye, 1)

            for n in range(2):
                slot_columns(n, n)
            for n in range(2):
                routed(n, n, True)
            with dve.Fori(1, SLOT_TILES // 2 - 1) as i:
                for n in range(2):
                    dve.wait_ge(s_rst[n], 16 * i)
                    routed(2 * i + n, n, True)
            for n in range(2):
                dve.wait_ge(s_rst[n], 16 * (SLOT_TILES // 2 - 1))
                routed(SLOT_TILES - 2 + n, n, False)
            dve.wait_ge(s_ry, SLOT_TILES)
            shared(1, sh_silu1, sh_h1)
            dve.wait_ge(s_ya, 2 * (B + 1))
            dve.wait_ge(s_gat, 16 * 2 * NT)
            for t in range(NT):
                r = tile_rows(t)
                link(nc.vector.scalar_tensor_tensor(out=h_res[0:r, t], in0=gat[0:r, 0, t], scalar=weight[0:r, 0, t:t + 1],
                                                    in1=h_res[0:r, t], op0=ALU.mult, op1=ALU.add))
                nc.vector.scalar_tensor_tensor(out=h_res[0:r, t], in0=gat[0:r, 1, t], scalar=weight[0:r, 1, t:t + 1],
                                               in1=h_res[0:r, t], op0=ALU.mult, op1=ALU.add).then_inc(s_fin, 1)

        @block.tensor
        def _(pe):
            mm = nc.tensor.matmul
            def tokens(step, r, w, first, last):
                for which in range(2):
                    pe.wait_ge(s_feat, 2 * RING + 2 * step + which + 1)
                    for j in range(HT_):
                        ins = mm(ps[:, j, 0:D], feat[r][:, which, j * P:(j + 1) * P], w(which),
                                 start=first and which == 0, stop=last and which == 1)
                ins.then_inc(s_used, 1)

            pe.wait_ge(s_wtok, 16)
            flat = w_tok_sb[:].rearrange("p s a d -> p (s a d)")
            for half in range(2):
                if half:
                    pe.wait_ge(s_hrow, HT_ * half)
                for k in range(BANDS):
                    tokens(half * STEPS + k, k % RING, lambda a: w_tok_sb[:, k, a], k == 0, False)
                with pe.Fori(1, XB) as c:
                    for k in range(BANDS):
                        tokens(half * STEPS + c * BANDS + k, k % RING,
                               lambda a: flat[:, bass.ds((c * BANDS + k) * 2 * D + a * D, D)], False, False)
                for k in range(BANDS // 2):
                    s = XB * BANDS + k
                    tokens(half * STEPS + s, k % RING, lambda a: w_tok_sb[:, s, a], False, k == BANDS // 2 - 1)

            def transposed_tokens(n):
                for t in range(NT):
                    r = tile_rows(t)
                    pe.wait_ge(s_xn, n * NT + t + 1)
                    if t >= 4:
                        pe.wait_ge(s_xnt, n * NT + t - 3)
                    for k in range(2):
                        ins = nc.tensor.transpose(ps[0:KH, t % 4, k * r:(k + 1) * r], xn[0:r, t, k * KH:(k + 1) * KH], ident[0:r, 0:r])
                    ins.then_inc(s_xnp, 1)

            pe.wait_ge(s_const, 16 * 7)
            pe.wait_ge(s_hrow, CLS)
            transposed_tokens(0)
            pe.wait_ge(s_attnw, 16 * 6)
            pe.wait_ge(s_xnt, NT)
            with pe.Fori(0, B) as b:
                for c in range(CH):
                    if c >= 2:
                        pe.wait_ge(s_qe, b * (CH + 1) + c - 1)
                    for k in range(2):
                        ins = mm(ps[:, c % 2, :], w_qkv_sb[:, k, c * P:(c + 1) * P], xn_t[:, k, bass.ds(b * SEQ, SEQ)],
                                 start=k == 0, stop=k == 1)
                    ins.then_inc(s_q, 1)
                for c in range(CH):
                    for k in range(2):
                        ins = mm(ps[:, 2, c:c + 1], w_qkv_sb[:, k, c * P:(c + 1) * P], xn_t[:, k, bass.ds(b + NX, 1)],
                                 start=k == 0, stop=k == 1)
                ins.then_inc(s_q, 1)
                pe.wait_ge(s_nl, b + 1)
                for c in range(CH):
                    mm(ps[0:NH, 3, :], norm_lhs[:, c], w_sq[:, c, 0:SEQ], start=c == 0, stop=c == CH - 1)
                for c in range(CH):
                    ins = mm(ps[0:NH, 2, 32:33], norm_lhs[:, c], w_sq[:, c, SEQ:SEQ + 1], start=c == 0, stop=c == CH - 1)
                ins.then_inc(s_lg, 1)
                pe.wait_ge(s_pi, b + 1)
                for c in range(CH):
                    if c >= 2:
                        pe.wait_ge(s_pbe, b * CH + c - 1)
                    mm(ps[:, 2, 64 + 2 * c:66 + 2 * c], spread_sb[:, c], pi[:, SEQ:SEQ + 2], start=True, stop=True)
                    mm(ps[:, c % 2, :], spread_sb[:, c], pi[:, 0:SEQ], start=True, stop=True).then_inc(s_pb, 1)
                pe.wait_ge(s_wo, 2 * b + 2)
                for c in range(CH):
                    for t in range(TPB):
                        ins = mm(ps[:, 4 + t, 0:D], wp[:, c, t * P:(t + 1) * P], w_out_b[:, c], start=c == 0, stop=c == CH - 1)
                ins.then_inc(s_y, 1)
                pe.wait_ge(s_ye, b + 1)
            for c in range(CH):
                ins = mm(ps[0:B, 0, 0:D], wp_cls[:, c], w_out_sb[:, c], start=c == 0, stop=c == CH - 1)
            ins.then_inc(s_y, 1)
            pe.wait_ge(s_ye, B + 1)
            transposed_tokens(1)
            pe.wait_ge(s_xnt, 2 * NT)
            for t in range(NT):
                r = tile_rows(t)
                for k in range(2):
                    ins = mm(ps[:, 4, t * NE:(t + 1) * NE] if r == P else ps[0:r, 4, t * NE:(t + 1) * NE],
                             xn_t[:, k, columns(t)], gate_sb[:, k], start=k == 0, stop=k == 1)
            ins.then_inc(s_rl, 1)
            pe.wait_ge(s_mask, 1)
            masks = mask[:].rearrange("p t e -> p (t e)")
            mm(ps[:, 4, 0:NT * NE], tri[:], masks, start=True, stop=True)
            mm(ps[:, 5, 0:NT * NE], ones[:], masks, start=True, stop=True).then_inc(s_cnt, 1)

            def shared(s, hidden):
                gu, dn = sh_gu_sb[s], sh_dn_sb[s]

                def block_(nth, tok, n):
                    def down(c):
                        pe.wait_ge(s_h, nth * FC + c + 1)
                        for t in range(-(-n // P)):
                            r = min(P, n - t * P)
                            ins = mm(ps[0:r, 4 + t, 0:D], hidden[:, c % 2, t * P:t * P + r], dn[:, c], start=c == 0, stop=c == FC - 1)
                        ins.then_inc(s_dn, 1)

                    for c in range(FC):
                        if c >= 2:
                            pe.wait_ge(s_h, nth * FC + c - 1)
                        for u in range(2):
                            for k in range(2):
                                ins = mm(ps[:, 2 * (c % 2) + u, 0:n], gu[:, k, u * FF + c * P:u * FF + (c + 1) * P],
                                         xn_t[:, k, tok], start=k == 0, stop=k == 1)
                        ins.then_inc(s_gu, 1)
                        if c >= 1:
                            down(c - 1)
                    down(FC - 1)

                pe.wait_ge(s_shw[s], 32)
                with pe.Fori(0, B) as b:
                    block_(s * (B + 1) + b, bass.ds(b * SEQ, SEQ), SEQ)
                    pe.wait_ge(s_ya, s * (B + 1) + b + 1)
                block_(s * (B + 1) + B, slice(NX, T), B)

            pe.wait_ge(s_te, 1)
            shared(0, sh_h)
            pe.wait_ge(s_ya, B + 1)
            pe.wait_ge(s_exw, 16 * 2 * NE)
            gu_flat = ex_gu_sb[:].rearrange("p e k n -> p (e k n)")
            dn_flat = ex_dn_sb[:].rearrange("p e c d -> p (e c d)")

            def slot_transposes(j, n, i):
                pe.wait_ge(s_sxe[n], 16 * (i + 1))
                for k in range(2):
                    ins = nc.tensor.transpose(ps[0:KH, 3 * n, k * P:(k + 1) * P], sx[:, n, k * KH:(k + 1) * KH], ident[:])
                ins.then_inc(s_xt, 1)

            def gate_up(j, n, e):
                pe.wait_ge(s_xte, j + 1)
                for q in range(2 * FF // 512):
                    for k in range(2):
                        ins = mm(ps[:, 3 * n + q, :], sx_t[n][:, k], gu_flat[:, bass.ds(e * (2 * 2 * FF) + (k * 2 * FF + q * 512), 512)],
                                 start=k == 0, stop=k == 1)
                ins.then_inc(s_rg, 1)

            def down(j, n, e, i, more):
                pe.wait_ge(s_rh, j + 1)
                for c in range(FC):
                    ins = nc.tensor.transpose(ps[:, 6 + c // 4, (c % 4) * P:(c % 4 + 1) * P], hid[:, n, c * P:(c + 1) * P], ident[:])
                ins.then_inc(s_ht, 1)
                if more:
                    slot_transposes(j + 2, n, i + 1)
                pe.wait_ge(s_hte, j + 1)
                for c in range(FC):
                    ins = mm(ps[:, 7, 256:256 + D], hid_t[n][:, c], dn_flat[:, bass.ds(e * (FC * D) + c * D, D)], start=c == 0, stop=c == FC - 1)
                ins.then_inc(s_ry, 1)
                pe.wait_ge(s_rye, j + 1)

            for n in range(2):
                slot_transposes(n, n, 0)
            with pe.Fori(0, SLOT_TILES // 2 - 1) as i:
                e = [pe.value_load(expert_i[0:1, bass.ds(2 * i + n, 1)], min_val=0, max_val=NE - 1) for n in range(2)]
                for n in range(2):
                    gate_up(2 * i + n, n, e[n])
                for n in range(2):
                    down(2 * i + n, n, e[n], i, True)
            for n in range(2):
                j = SLOT_TILES - 2 + n
                e = pe.value_load(expert_i[0:1, j:j + 1], min_val=0, max_val=NE - 1)
                gate_up(j, n, e)
                down(j, n, e, SLOT_TILES // 2 - 1, False)
            shared(1, sh_h1)


def _layouts(i):
    f = i["L0_tok_freq_bands"]
    w = i["L0_tok_W"].reshape(D, VALS, 2, BANDS).transpose(1, 3, 2, 0)
    full = w[:XB * P].reshape(XB, P, BANDS, 2, D).transpose(1, 0, 2, 3, 4).reshape(P, XB * BANDS, 2, D)
    left = w[XB * P:].reshape(LEFT, BANDS // 2, 2, 2, D).transpose(2, 0, 1, 3, 4).reshape(P, BANDS // 2, 2, D)

    def gate_up(g, u):
        both = np.concatenate([g, u], axis=1)
        return both.transpose(0, 2, 1).reshape(len(g), 2, KH, 2 * FF).transpose(0, 2, 1, 3)

    def down(d):
        return d.transpose(0, 2, 1).reshape(len(d), FC, P, D).transpose(0, 2, 1, 3)

    channel = np.arange(INNER)
    heads = (channel[:, None] // DH == np.arange(NH)).astype(np.float32)
    return {
        "x_t": i["x"].reshape(NX, VALS).T,
        "freqs": np.concatenate([np.tile(f, (P, 1)), np.repeat(f.reshape(BANDS // 2, 2), LEFT, axis=1).T], axis=1),
        "w_tok": np.concatenate([full, left], axis=1),
        "cls4": np.tile(i["cls_tok"].reshape(1, D), (B, 1)),
        "w_qkv": i["L0_attn_w_qkv"].reshape(2, KH, INNER).transpose(1, 0, 2),
        "temp": i["L0_attn_temp"],
        "w_out": i["L0_attn_w_out"].reshape(CH, P, D).transpose(1, 0, 2),
        "b_out": np.tile(i["L0_attn_b_out"], (P, 1)),
        "gate_t": i["L0_ffn_gate_w"].T.reshape(2, KH, NE).transpose(1, 0, 2),
        "sh_gu": gate_up(i["L0_ffn_shared_gate"], i["L0_ffn_shared_up"]),
        "sh_dn": down(i["L0_ffn_shared_down"]),
        "ex_gu": gate_up(i["L0_ffn_routed_gate"], i["L0_ffn_routed_up"]),
        "ex_dn": down(i["L0_ffn_routed_down"]),
        "c_ident": np.eye(P, dtype=np.float32),
        "c_tri": np.triu(np.ones((P, P), np.float32), 1),
        "c_heads": heads.reshape(CH, P, NH).transpose(1, 0, 2),
        "c_spread": heads.T.reshape(NH, CH, P),
        "c_iota": np.tile(np.concatenate([np.arange(SLOT_TILES), np.arange(NE)]).astype(np.float32), (P, 1)),
        "c_valid": (np.arange(P)[:, None] < np.where(np.arange(NT) < CLS, P, B)).astype(np.float32),
    }


def kernel(**inputs):
    import concourse.bacc as bacc
    from concourse.bass_utils import run_bass_kernel_spmd

    nc = bacc.Bacc("TRN2", target_bir_lowering=False, num_devices=1)
    arrays = {k: np.ascontiguousarray(v) for k, v in _layouts({k: np.asarray(v) for k, v in inputs.items()}).items()}
    args = {k: nc.dram_tensor(k, v.shape, F32, kind="ExternalInput").ap() for k, v in arrays.items()}
    args["out"] = nc.dram_tensor("out", (B, SEQ + 1, D), F32, kind="ExternalOutput").ap()
    args["slots_x"] = nc.dram_tensor("slots_x", (SLOTS, D), F32).ap()
    args["slots_y"] = nc.dram_tensor("slots_y", (SLOTS, D), F32).ap()
    vit_tower(nc, **args)
    result = run_bass_kernel_spmd(nc, [arrays], core_ids=[0])
    return result.results[0]["out"]
```

```python
from contextlib import ExitStack, contextmanager

import numpy as np

import concourse.bass as bass
from concourse import mybir

F32 = mybir.dt.float32
I32 = mybir.dt.int32
U32 = mybir.dt.uint32
ALU = mybir.AluOpType
ACT = mybir.ActivationFunctionType
AX_X = mybir.AxisListType.X

B, SEQ, D = 4, 512, 192
P = 128
NX = B * SEQ
NT = NX // P + 1
CLS = NT - 1
T = NX + B
TPB = SEQ // P
KH = D // 2
BANDS = 6
VALS = 3 * D
XB = VALS // P
LEFT = VALS - XB * P
STEPS = XB * BANDS + BANDS // 2
HALF = NX // 2
HT_ = HALF // P
NH, DH = 12, 64
INNER = NH * DH
CH = INNER // P
HPC = P // DH
NE, NS = 8, 2
FF = 768
FC = FF // P
EW = 2 * 2 * FF + FC * D
SLOT_TILES = (2 * T - NE) // P + NE
SLOTS = SLOT_TILES * P
EPS = 1e-5
RING = 3


class Chain:

    def __init__(self, eng, sem):
        self.eng, self.sem, self.count, self.loops = eng, sem, 0, 0

    def __call__(self, ins):
        ins.then_inc(self.sem, 1)
        self.count += 1
        self.eng.wait_ge(self.sem, self.count + self.loops)

    @contextmanager
    def loop(self, trips, links):
        before = self.loops
        with self.eng.Fori(0, trips) as i:
            self.loops = before + i * links
            first = self.count
            yield i
            assert self.count == first + links, (self.count - first, links)
        self.loops = before
        self.count += links * (trips - 1)


def vit_tower(nc, x_t, freqs, w_tok, cls4, w_qkv, temp, w_out, b_out, gate_t, sh_gu, sh_dn, ex_gu, ex_dn,
              c_ident, c_tri, c_heads, c_spread, c_iota, c_valid, out, slots_x, slots_y):
    ctx = ExitStack()
    base = -(-nc.sbuf_base // 32) * 32
    limit = nc.sbuf_base + nc.sbuf_bytes_remaining
    used = {}

    def at(name, shape, offset, dt=F32):
        size = -(-int(np.prod(shape[1:])) * 4 // 32) * 32
        used[name] = nc.alloc_sbuf_tensor_at(name, shape, dt, offset=offset)
        assert offset + size <= limit, (name, offset + size, limit)
        return used[name], offset + size

    with ctx:
        o = base
        h_res, o = at("h_res", [P, NT, D], o)
        xn_t, o = at("xn_t", [KH, 2, T], o)
        ident, o = at("ident", [P, P], o)
        ones, o = at("ones", [P, P], o)
        tri, o = at("tri", [P, P], o)
        stats, o = at("stats", [P, NT, 6], o)
        mean_var, o = at("mean_var", [P, NT, 2], o)
        std, o = at("std", [P, NT], o)
        rstd, o = at("rstd", [P, NT], o)
        gate_sb, o = at("gate_sb", [KH, 2, NE], o)
        iota_sb, o = at("iota_sb", [P, SLOT_TILES + NE], o)
        valid_sb, o = at("valid_sb", [P, NT], o)
        before, _ = at("before", [1, SLOT_TILES, NE], o)
        logit, o = at("logit", [P, NT, NE], o)
        score, o = at("score", [P, NT, NE], o)
        top, o = at("top", [P, NT, 8], o)
        top_at, o = at("top_at", [P, NT, 8], o, U32)
        top_f, o = at("top_f", [P, NT, 8], o)
        pick = []
        for j in range(2):
            t_, o = at(f"pick{j}", [P, NT, NE], o)
            pick.append(t_)
        mask, o = at("mask", [P, NT, NE], o)
        place, o = at("place", [P, NT, NE], o)
        total, o = at("total", [P, NT, NE], o)
        row, o = at("row", [P, 4, NT], o)
        weight, o = at("weight", [P, 2, NT], o)
        slot_f, o = at("slot_f", [P, NT], o)
        slot, o = at("slot", [P, 2, NT], o, I32)
        tiles_i, o = at("tiles_i", [P, NE], o, I32)
        tiles_f, o = at("tiles_f", [P, 3, NE], o)
        expert_f, o = at("expert_f", [1, SLOT_TILES], o)
        expert_i, o = at("expert_i", [1, SLOT_TILES], o, I32)
        half_pi, o = at("half_pi", [P, 1], o)
        eps_sb, o = at("eps_sb", [P, 1], o)
        experts_at = o
        rest_at = experts_at + NE * EW * 4

        o = experts_at
        x_sb, o = at("x_sb", [P, XB + 1, NX], o)
        w_tok_sb, o = at("w_tok_sb", [P, STEPS, 2, D], o)
        feat = []
        for r in range(RING):
            t_, o = at(f"feat{r}", [P, 2, HALF], o)
            feat.append(t_)
        turns, o = at("turns", [P, HALF], o, I32)
        phase = []
        for r in range(RING):
            t_, o = at(f"phase{r}", [P, 2, HALF], o)
            phase.append(t_)
        freq_sb, o = at("freq_sb", [P, BANDS + BANDS // 2], o)
        w_qkv_sb, o = at("w_qkv_sb", [KH, 2, INNER], o)
        w_out_sb, o = at("w_out_sb", [P, CH, D], o)
        heads_sb, o = at("heads_sb", [P, CH, NH], o)
        spread_sb, o = at("spread_sb", [NH, CH, P], o)
        temp_sb, o = at("temp_sb", [NH, 1], o)
        bias_sb, o = at("bias_sb", [P, D], o)
        assert o <= limit - NT * D * 4
        o = experts_at
        w_sb, o = at("w_sb", [P, 2, CH, SEQ + 1], o)
        w_sq, o = at("w_sq", [P, 2, CH, SEQ + 1], o)
        wp, o = at("wp", [P, CH, SEQ + 1], o)
        scratch, o = at("scratch", [P, SEQ], o)
        w_out_b, o = at("w_out_b", [P, CH, D], o)
        norm_sq, o = at("norm_sq", [P, CH], o)
        inv_sq, o = at("inv_sq", [P, CH], o)
        norm_lhs, o = at("norm_lhs", [P, CH, NH], o)
        lg, o = at("lg", [NH, SEQ + 1], o)
        pi, o = at("pi", [NH, SEQ + 2], o)
        soft, o = at("soft", [NH, 4], o)
        dots, o = at("dots", [P, CH], o)
        cls_dots, o = at("cls_dots", [P, CH], o)
        neg_attn, o = at("neg_attn", [P, CH], o)
        wp_cls, o = at("wp_cls", [P, CH, B], o)

        ex_gu_sb = nc.alloc_sbuf_tensor_at("ex_gu_sb", [KH, NE, 2, 2 * FF], F32, offset=experts_at)
        ex_dn_sb, o = at("ex_dn_sb", [P, NE, FC, D], experts_at + NE * 2 * 2 * FF * 4)
        assert o == rest_at
        xn_at = (limit - NT * D * 4) // 32 * 32
        xn, _ = at("xn", [P, NT, D], xn_at)
        zeros, _ = at("zeros", [P, 4, D], xn_at)
        sh_at = rest_at
        sh_gu_sb = [nc.alloc_sbuf_tensor_at("sh_gu0", [KH, 2, 2 * FF], F32, offset=sh_at), None]
        sh_dn0, o = at("sh_dn0", [P, FC, D], sh_at + 2 * 2 * FF * 4)
        sh_silu, o = at("sh_silu", [P, 2, SEQ], o)
        sh_h, o = at("sh_h", [P, 2, SEQ], o)
        assert o <= xn_at
        o = xn_at
        sx, o = at("sx", [P, 2, D], o)
        sx_t = [None, None]
        sx_t[0], o = at("sx_t0", [KH, 2, P], o)
        sx_t[1], o = at("sx_t1", [KH, 2, P], o)
        hid, o = at("hid", [P, 2, FF], o)
        sy, o = at("sy", [P, 2, D], o)
        o = rest_at
        sh_gu_sb[1], o = at("sh_gu1", [KH, 2, 2 * FF], o)
        sh_dn1, o = at("sh_dn1", [P, FC, D], o)
        sh_dn_sb = [sh_dn0, sh_dn1]
        hid_t = [None, None]
        hid_t[0], o = at("hid_t0", [P, FC, P], o)
        hid_t[1], o = at("hid_t1", [P, FC, P], o)
        assert o <= xn_at
        o = experts_at
        sh_silu1, o = at("sh_silu1", [P, 2, SEQ], o)
        sh_h1, o = at("sh_h1", [P, 2, SEQ], o)
        gat, o = at("gat", [P, 2, NT, D], o)

        ps = ctx.enter_context(nc.psum_tensor("ps", [P, 8, 512], F32))

        def sem(name):
            return ctx.enter_context(nc.semaphore(name))

        s_const = sem("constants_loaded")
        s_x = [sem(f"x_{name}_loaded") for name in ("first_block", "half0", "half1")]
        s_wtok = [sem(f"w_tok_{name}_loaded") for name in ("first", "rest")]
        s_freq = sem("frequencies_loaded")
        s_cls = sem("class_tokens_loaded")
        s_attnw = sem("attention_weights_loaded")
        s_zero = sem("zeros_ready")
        s_own = sem("vector_constants_ready")
        s_zeroed = sem("slots_zeroed")
        s_turns = sem("phases_ready")
        s_feat = sem("features_ready")
        s_used = sem("features_used")
        s_hrow = sem("token_rows_evacuated")
        s_dchain = sem("vector_chain")
        s_achain = sem("scalar_chain")
        s_var = sem("variances_ready")
        s_std = sem("deviations_ready")
        s_xn = sem("normalised_ready")
        s_xnp = sem("normalised_transposed")
        s_xnt = sem("normalised_columns_ready")
        s_hb = sem("bias_added")
        s_q = sem("projection_ready")
        s_qe = sem("projection_evacuated")
        s_nl = sem("norm_weights_ready")
        s_lg = sem("logits_ready")
        s_mx = sem("logit_maximum_ready")
        s_exp = sem("attention_exp_ready")
        s_pi = sem("pi_ready")
        s_pb = sem("pi_spread")
        s_pbe = sem("pi_spread_used")
        s_wo = sem("scaled_w_out_ready")
        s_y = sem("attention_out_ready")
        s_ye = sem("attention_out_added")
        s_rl = sem("router_logits_ready")
        s_rm = sem("router_maximum_taken")
        s_re = sem("router_exp_ready")
        s_mask = sem("mask_ready")
        s_cnt = sem("counts_ready")
        s_slot = sem("slots_ready")
        s_te = sem("tile_experts_ready")
        s_scat = sem("rows_scattered")
        s_shw = [sem(f"shared{i}_weights_loaded") for i in range(2)]
        s_exw = sem("expert_weights_loaded")
        s_gu = sem("shared_gate_up_ready")
        s_silu = sem("shared_silu_ready")
        s_h = sem("shared_hidden_ready")
        s_dn = sem("shared_hidden_used")
        s_ya = sem("shared_out_added")
        s_sx = sem("slot_rows_loaded")
        s_sxe = [sem(f"slot_rows_loaded{i}") for i in range(2)]
        s_xt = sem("slot_rows_transposed")
        s_xte = sem("slot_columns_ready")
        s_rg = sem("routed_gate_up_ready")
        s_rs = sem("routed_silu_ready")
        s_rh = sem("routed_hidden_ready")
        s_ht = sem("routed_hidden_transposed")
        s_hte = sem("routed_hidden_columns_ready")
        s_ry = sem("routed_out_ready")
        s_rye = sem("routed_out_evacuated")
        s_rst = [sem(f"routed_out_stored{i}") for i in range(2)]
        s_gat = [sem(f"rows_gathered{b}") for b in range(B + 1)]
        s_out = sem("out_stored")

        block = ctx.enter_context(nc.Block())

        def tile_rows(t):
            return P if t < CLS else B

        def columns(t):
            return slice(t * P, t * P + tile_rows(t))

        def tiles_of(group, last):
            own = [group * TPB + t for t in range(TPB)]
            return own + [CLS] if group == (B - 1 if last else 0) else own

        def order(n, group):
            return group * TPB + (group > 0 and n == 0)

        def bank(n, group, j):
            return 4 + (order(n, group) + j) % 4

        def y_tile(t, r=P):
            return ps[0:r, 4 + t // 2, (t % 2) * D:(t % 2 + 1) * D]

        @block.sync
        def _(sp):
            def load_x(blocks, cols, done):
                for c in blocks:
                    if c < XB:
                        sp.dma_start(x_sb[:, c, cols], x_t[c * P:(c + 1) * P, cols]).then_inc(done, 16)
                    else:
                        for part in range(P // LEFT):
                            sp.dma_start(x_sb[part * LEFT:(part + 1) * LEFT, XB, cols], x_t[XB * P:, cols]).then_inc(done, 16)

            sp.dma_start(freq_sb[:], freqs).then_inc(s_freq, 16)
            load_x([0], slice(0, HALF), s_x[0])
            load_x(range(1, XB + 1), slice(0, HALF), s_x[1])
            load_x(range(XB + 1), slice(HALF, NX), s_x[2])
            sp.dma_start(ident[:], c_ident).then_inc(s_const, 16)
            sp.dma_start(h_res[0:B, CLS, :], cls4).then_inc(s_cls, 16)
            sp.dma_start(tri[:], c_tri).then_inc(s_const, 16)
            sp.dma_start(gate_sb[:], gate_t).then_inc(s_const, 16)
            sp.dma_start(iota_sb[:], c_iota).then_inc(s_const, 16)
            sp.dma_start(valid_sb[:], c_valid).then_inc(s_const, 16)
            sp.dma_start(w_qkv_sb[:], w_qkv).then_inc(s_attnw, 16)
            sp.dma_start(w_out_sb[:], w_out).then_inc(s_attnw, 16)
            sp.dma_start(heads_sb[:], c_heads).then_inc(s_attnw, 16)
            sp.dma_start(spread_sb[:], c_spread).then_inc(s_attnw, 16)
            sp.dma_start(temp_sb[:], temp).then_inc(s_attnw, 16)
            sp.dma_start(bias_sb[:], b_out).then_inc(s_attnw, 16)
            sp.wait_ge(s_zero, 1)
            zero_rows = slots_x.rearrange("(n a p) d -> n p a d", p=P, a=4)
            for n in range(SLOT_TILES // 4):
                sp.dma_start(zero_rows[n], zeros[:]).then_inc(s_zeroed, 16)
            sp.wait_ge(s_ye, B + 2)
            sp.dma_start(sh_gu_sb[0][:], sh_gu[0]).then_inc(s_shw[0], 16)
            sp.dma_start(sh_dn_sb[0][:], sh_dn[0]).then_inc(s_shw[0], 16)
            for e in range(NE):
                sp.dma_start(ex_gu_sb[:, e], ex_gu[e]).then_inc(s_exw, 16)
                sp.dma_start(ex_dn_sb[:, e], ex_dn[e]).then_inc(s_exw, 16)
            sp.wait_ge(s_scat, 16 * 2 * NT)
            for n in range(2):
                sp.dma_start(sx[:, n], slots_x[n * P:(n + 1) * P, :]).then_inc(s_sxe[n], 16)
            sp.wait_ge(s_ya, B + 2)
            sp.dma_start(sh_gu_sb[1][:], sh_gu[1]).then_inc(s_shw[1], 16)
            sp.dma_start(sh_dn_sb[1][:], sh_dn[1]).then_inc(s_shw[1], 16)
            with sp.Fori(0, SLOT_TILES // 2 - 1) as i:
                for n in range(2):
                    sp.wait_ge(s_xt, 2 * i + n + 1)
                    sp.dma_start(sx[:, n], slots_x[bass.ds((2 * i + 2 + n) * P, P), :]).then_inc(s_sxe[n], 16)
            for b in range(B):
                sp.wait_ge(s_ya, (B + 2) + b + 1)
                sp.dma_start(out[b, 1:, :].rearrange("(t p) d -> p t d", p=P), h_res[:, b * TPB:(b + 1) * TPB, :]).then_inc(s_out, 16)
            sp.wait_ge(s_ya, 2 * (B + 1) + 1)
            sp.dma_start(out[:, 0, :], h_res[0:B, CLS, :]).then_inc(s_out, 16)
            sp.wait_ge(s_out, 16 * (B + 1))

        @block.gpsimd
        def _(pool):
            nc.gpsimd.memset(zeros[:], 0.0).then_inc(s_zero, 1)
            pool.wait_ge(s_attnw, 16 * 6)
            for g in range(B):
                pool.wait_ge(s_xn, g + 1)
                for t in tiles_of(g, False):
                    r = tile_rows(t)
                    nc.gpsimd.tensor_tensor(h_res[0:r, t], h_res[0:r, t], bias_sb[0:r, :], ALU.add).then_inc(s_hb, 1)
            pool.wait_ge(s_slot, 2)
            pool.wait_ge(s_zeroed, 16 * (SLOT_TILES // 4))
            for t in range(NT):
                r = tile_rows(t)
                for j in range(2):
                    nc.gpsimd.indirect_dma_start(
                        slots_x, bass.IndirectOffsetOnAxis(ap=slot[0:r, j, t:t + 1], axis=0),
                        xn[0:r, t, :], None).then_inc(s_scat, 16)
            for n in range(2):
                pool.wait_ge(s_rst[n], 16 * (SLOT_TILES // 2))
            pool.wait_ge(s_ry, SLOT_TILES)
            for t in range(NT):
                r = tile_rows(t)
                for j in range(2):
                    nc.gpsimd.indirect_dma_start(
                        gat[0:r, j, t, :], None, slots_y,
                        bass.IndirectOffsetOnAxis(ap=slot[0:r, j, t:t + 1], axis=0)).then_inc(s_gat[t // TPB], 16)

        @block.scalar
        def _(act):
            flat = w_tok_sb[:].rearrange("p s a d -> p (s a d)")
            flat_in = w_tok.rearrange("p s a d -> p (s a d)")
            cut = BANDS * 2 * D
            act.dma_start(flat[:, 0:cut], flat_in[:, 0:cut]).then_inc(s_wtok[0], 16)
            act.dma_start(flat[:, cut:], flat_in[:, cut:]).then_inc(s_wtok[1], 16)
            act.wait_ge(s_own, 1)

            def sines(step, r):
                act.wait_ge(s_turns, 2 * step + 2)
                act.wait_ge(s_used, step + 1)
                nc.scalar.activation(feat[r][:, 0], phase[r][:, 0], ACT.Sin, scale=6.283185).then_inc(s_feat, 1)
                nc.scalar.activation(feat[r][:, 1], phase[r][:, 1], ACT.Sin, bias=half_pi[:], scale=-6.283185).then_inc(s_feat, 1)

            def deviations(n, group):
                act.wait_ge(s_var, n * B + group + 1)
                first, own = group * TPB, tiles_of(group, n == 1)
                ins = nc.scalar.activation(std[:, first:first + TPB], mean_var[:, first:first + TPB, 1], ACT.Sqrt, bias=eps_sb[:])
                if CLS in own:
                    ins = nc.scalar.activation(std[0:B, CLS:CLS + 1], mean_var[0:B, CLS, 1:2], ACT.Sqrt, bias=eps_sb[0:B])
                ins.then_inc(s_std, 1)

            def norm_columns(n, group):
                for j, t in enumerate(tiles_of(group, n == 1)):
                    r = tile_rows(t)
                    act.wait_ge(s_xnp, n * NT + order(n, group) + j + 1)
                    nc.scalar.copy(xn_t[:, :, columns(t)], ps[0:KH, bank(n, group, j), 0:2 * r].rearrange("p (k n) -> p k n", k=2)).then_inc(s_xnt, 1)

            def attention_columns(b):
                for c in range(CH):
                    act.wait_ge(s_q, b * (CH + 1) + c + 1)
                    nc.scalar.copy(w_sb[:, bass.ds(b % 2, 1), c, 0:SEQ], ps[:, c % 2:c % 2 + 1, :])
                    nc.scalar.activation(w_sq[:, bass.ds(b % 2, 1), c, 0:SEQ], ps[:, c % 2:c % 2 + 1, :], ACT.Square,
                                         accum_out=norm_sq[:, c:c + 1]).then_inc(s_qe, 1)
                act.wait_ge(s_q, b * (CH + 1) + CH + 1)
                nc.scalar.copy(w_sb[:, bass.ds(b % 2, 1), :, SEQ], ps[:, 2:3, 0:CH])
                nc.scalar.activation(w_sq[:, bass.ds(b % 2, 1), :, SEQ], ps[:, 2:3, 0:CH], ACT.Square).then_inc(s_qe, 1)

            def exponentials(b):
                act.wait_ge(s_mx, b + 1)
                nc.scalar.activation(pi[:, 0:SEQ + 1], lg[:], ACT.Exp, bias=soft[:, 0:1], accum_out=soft[:, 1:2]).then_inc(s_exp, 1)

            for half in range(2):
                for k in range(BANDS):
                    sines(half * STEPS + k, k % RING)
                if half:
                    deviations(0, 0)
                    deviations(0, 1)
                with act.Fori(1, XB) as c:
                    for k in range(BANDS):
                        sines(half * STEPS + c * BANDS + k, k % RING)
                for k in range(BANDS // 2):
                    sines(half * STEPS + XB * BANDS + k, k % RING)
                act.wait_ge(s_used, half * STEPS + STEPS + RING)
                for j in range(HT_):
                    nc.scalar.copy(h_res[:, half * HT_ + j, :], ps[:, j, 0:D]).then_inc(s_hrow, 1)
            deviations(0, 2)
            norm_columns(0, 0)
            deviations(0, 3)
            norm_columns(0, 1)
            attention_columns(0)
            norm_columns(0, 2)
            norm_columns(0, 3)
            with act.Fori(0, B - 1) as b:
                exponentials(b)
                attention_columns(b + 1)
            exponentials(B - 1)
            for g in range(B):
                deviations(1, g)
                if g >= 1:
                    norm_columns(1, g - 1)
            norm_columns(1, B - 1)
            act.wait_ge(s_rm, 1)
            nc.scalar.activation(score[:], logit[:], ACT.Exp).then_inc(s_re, 1)

            def shared(s, silu):
                def block_(first, n):
                    for c in range(FC):
                        act.wait_ge(s_gu, first + c + 1)
                        nc.scalar.activation(silu[:, c % 2, 0:n], ps[:, 2 * (c % 2), 0:n], ACT.Silu).then_inc(s_silu, 1)
                with act.Fori(0, B) as b:
                    block_((s * (B + 1) + b) * FC, SEQ)
                block_((s * (B + 1) + B) * FC, B)

            shared(0, sh_silu)
            def silu(j, n):
                act.wait_ge(s_rg, j + 1)
                nc.scalar.activation(hid[:, n, :], ps[:, 3 * n:3 * n + 3, :].rearrange("p a n -> p (a n)")[:, 0:FF], ACT.Silu).then_inc(s_rs, 1)

            def hidden_columns(j, n):
                act.wait_ge(s_ht, j + 1)
                nc.scalar.copy(hid_t[n][:], ps[:, 6:8, :].rearrange("p a n -> p (a n)")[:, 0:FF].rearrange("p (c n) -> p c n", c=FC)).then_inc(s_hte, 1)

            def store(j, n):
                act.wait_ge(s_rye, j + 2)
                act.dma_start(slots_y[bass.ds(j * P, P), :], sy[:, n]).then_inc(s_rst[n], 16)

            silu(0, 0)
            hidden_columns(0, 0)
            silu(1, 1)
            store(0, 0)
            with act.Fori(1, SLOT_TILES // 2) as i:
                for n in range(2):
                    hidden_columns(2 * i + n - 1, 1 - n)
                    silu(2 * i + n, n)
                    store(2 * i + n - 1, 1 - n)
            hidden_columns(SLOT_TILES - 1, 1)
            store(SLOT_TILES - 1, 1)
            act.wait_ge(s_ry, SLOT_TILES)
            shared(1, sh_silu1)

        @block.vector
        def _(dve):
            link = Chain(dve, s_dchain)
            nc.vector.memset(half_pi[:], float(np.pi / 2))
            nc.vector.memset(eps_sb[:], EPS)
            nc.vector.memset(ones[:], 1.0).then_inc(s_used, RING)
            nc.vector.memset(std[:], 1.0).then_inc(s_feat, 2 * RING)
            nc.vector.memset(rstd[:], 1.0).then_inc(s_ye, 1)
            nc.vector.memset(score[:], 0.0).then_inc(s_ya, 1)
            nc.vector.memset(top[:], 0.0).then_inc(s_rye, 1)
            nc.vector.memset(logit[:], 0.0).then_inc(s_dn, 2)
            nc.vector.memset(mean_var[:], 1.0).then_inc(s_own, 1)
            dve.wait_ge(s_own, 1)

            def phases(step, r, x, f):
                link(nc.vector.tensor_scalar(turns[:], x, freq_sb[:, f:f + 1], None, ALU.mult))
                dve.wait_ge(s_feat, 2 * step + 2)
                nc.vector.scalar_tensor_tensor(out=phase[r][:, 0], in0=x, scalar=freq_sb[:, f:f + 1], in1=turns[:],
                                               op0=ALU.mult, op1=ALU.subtract).then_inc(s_turns, 1)
                dve.wait_ge(s_turns, 2 * step + 1)
                nc.vector.tensor_scalar(phase[r][:, 1].bitcast(I32), phase[r][:, 0].bitcast(I32), 0x7FFFFFFF, None,
                                        ALU.bitwise_and).then_inc(s_turns, 1)

            dve.wait_ge(s_freq, 16)
            def deviation_inputs(n, group):
                own = tiles_of(group, n == 1)
                for t in own:
                    if n == 0 or t == CLS:
                        r = tile_rows(t)
                        last = nc.vector.bn_stats(stats[0:r, t], h_res[0:r, t, :])
                if n == 0 or CLS in own:
                    link(last)
                for t in own:
                    r = tile_rows(t)
                    last = nc.vector.bn_aggr(mean_var[0:r, t], stats[0:r, t])
                last.then_inc(s_var, 1)

            def normalise(n, group):
                own = tiles_of(group, n == 1)
                dve.wait_ge(s_std, n * B + group + 1)
                first = group * TPB
                if CLS in own:
                    nc.vector.reciprocal(rstd[0:B, CLS:CLS + 1], std[0:B, CLS:CLS + 1])
                link(nc.vector.reciprocal(rstd[:, first:first + TPB], std[:, first:first + TPB]))
                for t in own:
                    r = tile_rows(t)
                    last = nc.vector.tensor_scalar(xn[0:r, t], h_res[0:r, t, :], mean_var[0:r, t, 0:1], rstd[0:r, t:t + 1],
                                                   ALU.subtract, ALU.mult)
                last.then_inc(s_xn, 1)

            for half in range(2):
                cols = slice(half * HALF, (half + 1) * HALF)
                dve.wait_ge(s_x[2 * half], 16 if half == 0 else 16 * (XB + 2))
                for k in range(BANDS):
                    phases(half * STEPS + k, k % RING, x_sb[:, 0, cols], k)
                if half:
                    dve.wait_ge(s_hrow, HT_)
                    dve.wait_ge(s_cls, 16)
                    deviation_inputs(0, 0)
                    deviation_inputs(0, 1)
                else:
                    dve.wait_ge(s_x[1], 16 * (XB + 1))
                with link.loop(XB - 1, BANDS) as i:
                    for k in range(BANDS):
                        phases(half * STEPS + (i + 1) * BANDS + k, k % RING, x_sb[:, bass.ds(i + 1, 1), cols].rearrange("p a n -> p (a n)"), k)
                if half:
                    dve.wait_ge(s_zeroed, 16 * (SLOT_TILES // 4))
                    normalise(0, 0)
                    normalise(0, 1)
                for k in range(BANDS // 2):
                    phases(half * STEPS + XB * BANDS + k, k % RING, x_sb[:, XB, cols], BANDS + k)
            dve.wait_ge(s_hrow, CLS)
            deviation_inputs(0, 2)
            deviation_inputs(0, 3)
            normalise(0, 2)
            normalise(0, 3)
            dve.wait_ge(s_attnw, 16 * 6)

            def norms(b):
                dve.wait_ge(s_qe, b * (CH + 1) + CH + 1)
                link(nc.vector.tensor_tensor(norm_sq[:], norm_sq[:], w_sq[:, bass.ds(b % 2, 1), :, SEQ].rearrange("p a c -> p (a c)"), ALU.add))
                link(nc.vector.tensor_scalar(norm_sq[:], norm_sq[:], 1e-24, None, ALU.max))
                link(nc.vector.reciprocal(inv_sq[:], norm_sq[:]))
                nc.vector.tensor_tensor(norm_lhs[:], heads_sb[:], inv_sq[:].rearrange("p (c a) -> p c a", a=1).to_broadcast([P, CH, NH]),
                                        ALU.mult).then_inc(s_nl, 1)

            def attend(b):
                w = w_sb[:, bass.ds(b % 2, 1)].rearrange("p a c n -> p (a c) n")
                dve.wait_ge(s_lg, b + 1)
                nc.vector.tensor_scalar(lg[:, 0:SEQ], ps[0:NH, 3, :], temp_sb[:], None, ALU.mult)
                link(nc.vector.tensor_scalar(lg[:, SEQ:SEQ + 1], ps[0:NH, 2, 32:33], temp_sb[:], None, ALU.mult))
                nc.vector.tensor_reduce(soft[:, 0:1], lg[:], AX_X, ALU.max, negate=True).then_inc(s_mx, 1)
                dve.wait_ge(s_exp, b + 1)
                link(nc.vector.reciprocal(soft[:, 2:3], soft[:, 1:2]))
                link(nc.vector.tensor_scalar(pi[:, 0:SEQ + 1], pi[:, 0:SEQ + 1], soft[:, 2:3], None, ALU.mult))
                link(nc.vector.tensor_reduce(soft[:, 3:4], pi[:, 0:SEQ + 1], AX_X, ALU.add))
                link(nc.vector.tensor_scalar(soft[:, 3:4], soft[:, 3:4], 1e-8, None, ALU.add))
                nc.vector.reciprocal(pi[:, SEQ + 1:SEQ + 2], soft[:, 3:4]).then_inc(s_pi, 1)
                for c in range(CH):
                    dve.wait_ge(s_pb, b * CH + c + 1)
                    link(nc.vector.tensor_tensor(wp[:, c, 0:SEQ], ps[:, 6 + c % 2, :], w[:, c, 0:SEQ], ALU.mult))
                    nc.vector.scalar_tensor_tensor(out=scratch[:], in0=wp[:, c, 0:SEQ], scalar=1.0, in1=w[:, c, 0:SEQ],
                                                   op0=ALU.mult, op1=ALU.mult, accum_out=dots[:, c:c + 1]).then_inc(s_pbe, 1)
                spread = ps[:, 3, 0:2 * CH].rearrange("p (c a) -> p c a", a=2)
                link(nc.vector.tensor_tensor(wp[:, :, SEQ], spread[:, :, 0], w[:, :, SEQ], ALU.mult))
                link(nc.vector.tensor_tensor(cls_dots[:], wp[:, :, SEQ], w[:, :, SEQ], ALU.mult))
                dve.wait_ge(s_pbe, b * CH + CH)
                link(nc.vector.tensor_tensor(dots[:], dots[:], cls_dots[:], ALU.add))
                link(nc.vector.tensor_tensor(dots[:], dots[:], spread[:, :, 1], ALU.mult))
                link(nc.vector.tensor_scalar(dots[:], dots[:], 1.0, -1.0, ALU.add, ALU.mult))
                nc.vector.reciprocal(neg_attn[:], dots[:]).then_inc(s_wo, 1)
                dve.wait_ge(s_wo, 2 * b + 1)
                nc.vector.tensor_tensor(wp_cls[:, :, bass.ds(b, 1)].rearrange("p c a -> p (c a)"), wp[:, :, SEQ], neg_attn[:], ALU.mult)
                nc.vector.tensor_tensor(w_out_b[:], w_out_sb[:], neg_attn[:].rearrange("p (c a) -> p c a", a=1).to_broadcast([P, CH, D]),
                                        ALU.mult).then_inc(s_wo, 1)

            def attended(b):
                dve.wait_ge(s_y, b + 1)
                for t in range(TPB):
                    last = nc.vector.tensor_tensor(h_res[:, bass.ds(b * TPB + t, 1), :], y_tile(t).rearrange("p (a d) -> p a d", a=1),
                                                   h_res[:, bass.ds(b * TPB + t, 1), :], ALU.add)
                last.then_inc(s_ye, 1)
                dve.wait_ge(s_ye, b + 2)
                for t in range(TPB):
                    last = nc.vector.bn_stats(stats[:, bass.ds(b * TPB + t, 1)].rearrange("p a s -> p (a s)"),
                                              h_res[:, bass.ds(b * TPB + t, 1), :].rearrange("p a d -> p (a d)"))
                link(last)

            dve.wait_ge(s_hb, NT)
            norms(0)
            with link.loop(B - 1, 19 + 1) as b:
                attend(b)
                norms(b + 1)
                attended(b)
            attend(B - 1)
            attended(B - 1)
            for g in range(B - 1):
                deviation_inputs(1, g)
            dve.wait_ge(s_y, B + 1)
            nc.vector.tensor_tensor(h_res[0:B, CLS, :], ps[0:B, 0, 0:D], h_res[0:B, CLS, :], ALU.add).then_inc(s_ye, 1)
            dve.wait_ge(s_ye, B + 2)
            deviation_inputs(1, B - 1)
            for g in range(B):
                normalise(1, g)

            dve.wait_ge(s_rl, 1)
            lg_ps = ps[:, 3, 0:NT * NE].rearrange("p (t e) -> p t e", e=NE)

            def over_experts(x):
                return x.rearrange("p (t a) -> p t a", a=1).to_broadcast([P, NT, NE])

            link(nc.vector.tensor_reduce(row[:, 0], lg_ps, AX_X, ALU.max))
            nc.vector.tensor_tensor(logit[:], lg_ps, over_experts(row[:, 0]), ALU.subtract).then_inc(s_rm, 1)
            dve.wait_ge(s_re, 1)
            link(nc.vector.tensor_reduce(row[:, 1], score[:], AX_X, ALU.add))
            link(nc.vector.reciprocal(row[:, 2], row[:, 1]))
            link(nc.vector.tensor_tensor(score[:], score[:], over_experts(row[:, 2]), ALU.mult))

            def best_scores():
                for t in range(NT):
                    last = nc.vector.max(top[:, t], score[:, t])
                link(last)

            def best_experts():
                for t in range(NT):
                    last = nc.vector.max_index(top_at[:, t], top[:, t], score[:, t])
                link(last)
                link(nc.vector.tensor_copy(top_f[:], top_at[:]))

            def picks():
                experts_row = iota_sb[:, SLOT_TILES:].rearrange("p (a e) -> p a e", a=1).to_broadcast([P, NT, NE])
                for j in range(2):
                    link(nc.vector.tensor_tensor(pick[j][:], experts_row, top_f[:, :, j:j + 1].to_broadcast([P, NT, NE]), ALU.is_equal))
                    link(nc.vector.tensor_tensor(pick[j][:], pick[j][:], over_experts(valid_sb[:]), ALU.mult))
                nc.vector.tensor_tensor(mask[:], pick[0][:], pick[1][:], ALU.add).then_inc(s_mask, 1)
                link(nc.vector.tensor_tensor(row[:, 3], top[:, :, 0], top[:, :, 1], ALU.add))
                link(nc.vector.tensor_scalar(row[:, 3], row[:, 3], 1e-8, None, ALU.add))
                link(nc.vector.reciprocal(row[:, 0], row[:, 3]))
                for j in range(2):
                    last = nc.vector.tensor_tensor(weight[:, j], top[:, :, j], row[:, 0], ALU.mult)
                link(last)

            def places():
                dve.wait_ge(s_cnt, 1)
                in_tile = ps[:, 6, 0:NT * NE].rearrange("p (t e) -> p t e", e=NE)
                of_tile = ps[:, 7, 0:NT * NE].rearrange("p (t e) -> p t e", e=NE)
                link(nc.vector.tensor_copy(place[:], of_tile))
                for e in range(NE):
                    last = nc.vector.tensor_tensor_scan(total[:, :, e], ones[:, 0:NT], place[:, :, e], 0.0, ALU.mult, ALU.add)
                link(last)
                link(nc.vector.tensor_tensor(place[:], total[:], place[:], ALU.subtract))
                link(nc.vector.tensor_tensor(place[:], place[:], in_tile, ALU.add))
                link(nc.vector.tensor_scalar(tiles_i[:], total[:, CLS], 1.0 / P, 0.5 - 0.5 / P, ALU.mult, ALU.add))
                link(nc.vector.tensor_copy(tiles_f[:, 0], tiles_i[:]))
                link(nc.vector.tensor_tensor_scan(tiles_f[:, 1], ones[:, 0:NE], tiles_f[:, 0], 0.0, ALU.mult, ALU.add))
                link(nc.vector.tensor_tensor(tiles_f[:, 2], tiles_f[:, 1], tiles_f[:, 0], ALU.subtract))
                link(nc.vector.tensor_scalar(tiles_f[:, 2], tiles_f[:, 2], float(P), None, ALU.mult))

            def slots():
                link(nc.vector.tensor_tensor(place[:], place[:], tiles_f[:, 2:3].to_broadcast([P, NT, NE]), ALU.add))
                for j in range(2):
                    link(nc.vector.tensor_tensor(pick[j][:], pick[j][:], place[:], ALU.mult))
                    link(nc.vector.tensor_reduce(slot_f[:], pick[j][:], AX_X, ALU.add))
                    nc.vector.tensor_copy(slot[:, j], slot_f[:]).then_inc(s_slot, 1)
                    dve.wait_ge(s_slot, j + 1)
                link(nc.vector.tensor_tensor(before[:], tiles_f[0:1, 1:2].to_broadcast([1, SLOT_TILES, NE]),
                                             iota_sb[0:1, 0:SLOT_TILES].rearrange("p (t a) -> p t a", a=1).to_broadcast([1, SLOT_TILES, NE]), ALU.is_le))
                link(nc.vector.tensor_reduce(expert_f[:], before[:], AX_X, ALU.add))
                nc.vector.tensor_scalar(expert_i[:], expert_f[:], float(NE - 1), None, ALU.min).then_inc(s_te, 1)

            def hidden_chunk(nth, c, n, silu, hidden):
                dve.wait_ge(s_silu, nth * FC + c + 1)
                dve.wait_ge(s_dn, nth * FC + c + 1)
                nc.vector.tensor_tensor(hidden[:, c % 2, 0:n], silu[:, c % 2, 0:n], ps[:, 2 * (c % 2) + 1, 0:n],
                                        ALU.mult).then_inc(s_h, 1)

            def shared_out(nth, b, own):
                dve.wait_ge(s_dn, nth * FC + FC + 2)
                for t in range(own):
                    if own == 1:
                        h, y = h_res[0:B, CLS, :], y_tile(0, B)
                    else:
                        h, y = h_res[:, bass.ds(b * TPB + t, 1), :], y_tile(t).rearrange("p (a d) -> p a d", a=1)
                    last = nc.vector.scalar_tensor_tensor(out=h, in0=y, scalar=1.0 / NS, in1=h, op0=ALU.mult, op1=ALU.add)
                last.then_inc(s_ya, 1)

            for c in range(FC):
                hidden_chunk(0, c, SEQ, sh_silu, sh_h)
                if c == 0:
                    best_scores()
                if c == 1:
                    best_experts()
                if c == 2:
                    picks()
                if c == 4:
                    places()
            shared_out(0, 0, TPB)
            slots()
            with dve.Fori(1, B) as b:
                for c in range(FC):
                    hidden_chunk(b, c, SEQ, sh_silu, sh_h)
                shared_out(b, b, TPB)
            for c in range(FC):
                hidden_chunk(B, c, B, sh_silu, sh_h)
            shared_out(B, 0, 1)

            dve.wait_ge(s_scat, 16 * 2 * NT)

            def slot_columns(j, n):
                dve.wait_ge(s_xt, j + 1)
                nc.vector.tensor_copy(sx_t[n][:], ps[0:KH, 3 * n, 0:2 * P].rearrange("p (k n) -> p k n", k=2)).then_inc(s_xte, 1)

            def routed_hidden(j, n):
                dve.wait_ge(s_rs, j + 1)
                up = ps[:, 3 * n:3 * n + 3, :].rearrange("p a n -> p (a n)")[:, FF:2 * FF]
                nc.vector.tensor_tensor(hid[:, n], hid[:, n], up, ALU.mult).then_inc(s_rh, 1)

            def routed_out(j, n):
                dve.wait_ge(s_ry, j + 1)
                nc.vector.tensor_copy(sy[:, n], ps[:, 7, 256:256 + D]).then_inc(s_rye, 1)

            slot_columns(0, 0)
            slot_columns(1, 1)
            routed_hidden(0, 0)
            for n in range(2):
                slot_columns(2 + n, n)
                routed_hidden(1 + n, 1 - n)
                routed_out(n, n)
            with dve.Fori(1, SLOT_TILES // 2 - 1) as i:
                for n in range(2):
                    slot_columns(2 * i + 2 + n, n)
                    routed_hidden(2 * i + 1 + n, 1 - n)
                    dve.wait_ge(s_rst[n], 16 * i)
                    routed_out(2 * i + n, n)
            routed_hidden(SLOT_TILES - 1, 1)
            for n in range(2):
                dve.wait_ge(s_rst[n], 16 * (SLOT_TILES // 2 - 1))
                routed_out(SLOT_TILES - 2 + n, n)

            dve.wait_ge(s_ry, SLOT_TILES)
            for b in range(B + 1):
                own = [b * TPB + t for t in range(TPB)] if b < B else [CLS]
                n = SEQ if b < B else B
                for c in range(FC):
                    hidden_chunk(B + 1 + b, c, n, sh_silu1, sh_h1)
                    if c == 2:
                        dve.wait_ge(s_gat[b], 16 * 2 * len(own))
                    if c in (2, 4):
                        for t in own:
                            r, j = tile_rows(t), c // 2 - 1
                            last = nc.vector.scalar_tensor_tensor(out=h_res[0:r, t], in0=gat[0:r, j, t], scalar=weight[0:r, j, t:t + 1],
                                                                  in1=h_res[0:r, t], op0=ALU.mult, op1=ALU.add)
                        link(last)
                shared_out(B + 1 + b, b, len(own))

        @block.tensor
        def _(pe):
            mm = nc.tensor.matmul
            def tokens(step, r, w, first, last):
                for which in range(2):
                    pe.wait_ge(s_feat, 2 * RING + 2 * step + which + 1)
                    for j in range(HT_):
                        ins = mm(ps[:, j, 0:D], feat[r][:, which, j * P:(j + 1) * P], w(which),
                                 start=first and which == 0, stop=last and which == 1)
                ins.then_inc(s_used, 1)

            flat = w_tok_sb[:].rearrange("p s a d -> p (s a d)")
            for half in range(2):
                if half == 0:
                    pe.wait_ge(s_wtok[0], 16)
                else:
                    pe.wait_ge(s_hrow, HT_ * half)
                for k in range(BANDS):
                    tokens(half * STEPS + k, k % RING, lambda a: w_tok_sb[:, k, a], k == 0, False)
                if half == 0:
                    pe.wait_ge(s_wtok[1], 16)
                with pe.Fori(1, XB) as c:
                    for k in range(BANDS):
                        tokens(half * STEPS + c * BANDS + k, k % RING,
                               lambda a: flat[:, bass.ds((c * BANDS + k) * 2 * D + a * D, D)], False, False)
                for k in range(BANDS // 2):
                    s = XB * BANDS + k
                    tokens(half * STEPS + s, k % RING, lambda a: w_tok_sb[:, s, a], False, k == BANDS // 2 - 1)

            def transposed_tokens(n, group):
                pe.wait_ge(s_xn, n * B + group + 1)
                for j, t in enumerate(tiles_of(group, n == 1)):
                    r, at_ = tile_rows(t), order(n, group) + j
                    if at_ >= 4:
                        pe.wait_ge(s_xnt, n * NT + at_ - 3)
                    for k in range(2):
                        ins = nc.tensor.transpose(ps[0:KH, bank(n, group, j), k * r:(k + 1) * r], xn[0:r, t, k * KH:(k + 1) * KH], ident[0:r, 0:r])
                    ins.then_inc(s_xnp, 1)

            def project(b, chunks):
                for c in chunks:
                    if c >= 2:
                        pe.wait_ge(s_qe, b * (CH + 1) + c - 1)
                    for k in range(2):
                        ins = mm(ps[:, c % 2, :], w_qkv_sb[:, k, c * P:(c + 1) * P], xn_t[:, k, bass.ds(b * SEQ, SEQ)],
                                 start=k == 0, stop=k == 1)
                    ins.then_inc(s_q, 1)

            def project_class(b):
                for c in range(CH):
                    for k in range(2):
                        ins = mm(ps[:, 2, c:c + 1], w_qkv_sb[:, k, c * P:(c + 1) * P], xn_t[:, k, bass.ds(b + NX, 1)],
                                 start=k == 0, stop=k == 1)
                ins.then_inc(s_q, 1)

            def logits(b):
                pe.wait_ge(s_nl, b + 1)
                half_ = bass.ds(b % 2, 1)
                for c in range(CH):
                    mm(ps[0:NH, 3, :], norm_lhs[:, c], w_sq[:, half_, c, 0:SEQ], start=c == 0, stop=c == CH - 1)
                for c in range(CH):
                    ins = mm(ps[0:NH, 2, 32:33], norm_lhs[:, c], w_sq[:, half_, c, SEQ:SEQ + 1], start=c == 0, stop=c == CH - 1)
                ins.then_inc(s_lg, 1)

            def spread_pi(b):
                pe.wait_ge(s_pi, b + 1)
                for c in range(CH):
                    if c >= 2:
                        pe.wait_ge(s_pbe, b * CH + c - 1)
                    mm(ps[:, 3, 2 * c:2 * c + 2], spread_sb[:, c], pi[:, SEQ:SEQ + 2], start=True, stop=True)
                    mm(ps[:, 6 + c % 2, :], spread_sb[:, c], pi[:, 0:SEQ], start=True, stop=True).then_inc(s_pb, 1)

            def attention_out(b):
                pe.wait_ge(s_wo, 2 * b + 2)
                pe.wait_ge(s_ye, b + 1)
                for c in range(CH):
                    for t in range(TPB):
                        ins = mm(y_tile(t), wp[:, c, t * P:(t + 1) * P], w_out_b[:, c], start=c == 0 and t % 2 == 0, stop=c == CH - 1,
                                 skip_group_check=True)
                ins.then_inc(s_y, 1)

            pe.wait_ge(s_const, 16 * 5)
            for j in range(4, HT_):
                pe.wait_ge(s_hrow, HT_ + j + 1)
            transposed_tokens(0, 0)
            transposed_tokens(0, 1)
            pe.wait_ge(s_attnw, 16 * 6)
            pe.wait_ge(s_xnt, TPB + 1)
            project(0, range(CH))
            project_class(0)
            transposed_tokens(0, 2)
            transposed_tokens(0, 3)
            pe.wait_ge(s_xnt, NT)
            with pe.Fori(0, B - 1) as b:
                logits(b)
                pe.wait_ge(s_qe, (b + 1) * (CH + 1))
                project(b + 1, range(CH // 2))
                spread_pi(b)
                project(b + 1, range(CH // 2, CH))
                pe.wait_ge(s_mx, b + 1)
                project_class(b + 1)
                attention_out(b)
            logits(B - 1)
            spread_pi(B - 1)
            attention_out(B - 1)
            for c in range(CH):
                ins = mm(ps[0:B, 0, 0:D], wp_cls[:, c], w_out_sb[:, c], start=c == 0, stop=c == CH - 1)
            ins.then_inc(s_y, 1)

            def router_logits(group):
                own = tiles_of(group, True)
                pe.wait_ge(s_xnt, NT + order(1, group) + len(own))
                for t in own:
                    r = tile_rows(t)
                    for k in range(2):
                        ins = mm(ps[0:r, 3, t * NE:(t + 1) * NE], xn_t[:, k, columns(t)], gate_sb[:, k], start=k == 0, stop=k == 1)
                if group == B - 1:
                    ins.then_inc(s_rl, 1)

            pe.wait_ge(s_ye, B + 2)
            transposed_tokens(1, 0)
            for g in range(1, B):
                transposed_tokens(1, g)
                router_logits(g - 1)
            router_logits(B - 1)

            def shared_gate_up(nth, c, s, tok, n):
                if c >= 2:
                    pe.wait_ge(s_h, nth * FC + c - 1)
                for u in range(2):
                    for k in range(2):
                        ins = mm(ps[:, 2 * (c % 2) + u, 0:n], sh_gu_sb[s][:, k, u * FF + c * P:u * FF + (c + 1) * P],
                                 xn_t[:, k, tok], start=k == 0, stop=k == 1)
                ins.then_inc(s_gu, 1)

            def shared_down(nth, c, s, n, hidden):
                pe.wait_ge(s_h, nth * FC + c + 1)
                if c == 0:
                    pe.wait_ge(s_ya, nth + 1)
                for t in range(-(-n // P)):
                    r = min(P, n - t * P)
                    ins = mm(y_tile(t, r), hidden[:, c % 2, t * P:t * P + r], sh_dn_sb[s][:, c], start=c == 0 and t % 2 == 0, stop=c == FC - 1,
                             skip_group_check=True)
                ins.then_inc(s_dn, 1)

            def shared_block(nth, s, tok, n, hidden):
                shared_gate_up(nth, 0, s, tok, n)
                for c in range(1, FC):
                    shared_gate_up(nth, c, s, tok, n)
                    shared_down(nth, c - 1, s, n, hidden)
                shared_down(nth, FC - 1, s, n, hidden)

            pe.wait_ge(s_shw[0], 32)
            pe.wait_ge(s_rm, 1)
            shared_gate_up(0, 0, 0, slice(0, SEQ), SEQ)
            for c in range(1, FC):
                shared_gate_up(0, c, 0, slice(0, SEQ), SEQ)
                shared_down(0, c - 1, 0, SEQ, sh_h)
                if c == 4:
                    pe.wait_ge(s_mask, 1)
                    masks = mask[:].rearrange("p t e -> p (t e)")
                    mm(ps[:, 6, 0:NT * NE], tri[:], masks, start=True, stop=True)
                    mm(ps[:, 7, 0:NT * NE], ones[:], masks, start=True, stop=True).then_inc(s_cnt, 1)
            shared_down(0, FC - 1, 0, SEQ, sh_h)
            with pe.Fori(1, B) as b:
                pe.wait_ge(s_h, b * FC)
                shared_block(b, 0, bass.ds(b * SEQ, SEQ), SEQ, sh_h)
            pe.wait_ge(s_h, B * FC)
            shared_block(B, 0, slice(NX, T), B, sh_h)

            pe.wait_ge(s_ya, B + 2)
            pe.wait_ge(s_te, 1)
            pe.wait_ge(s_exw, 16 * 2 * NE)
            gu_flat = ex_gu_sb[:].rearrange("p e k n -> p (e k n)")
            dn_flat = ex_dn_sb[:].rearrange("p e c d -> p (e c d)")

            def expert_of(j):
                return pe.value_load(expert_i[0:1, bass.ds(j, 1)], min_val=0, max_val=NE - 1)

            def slot_transposes(n, loads):
                pe.wait_ge(s_sxe[n], 16 * loads)
                for k in range(2):
                    ins = nc.tensor.transpose(ps[0:KH, 3 * n, k * P:(k + 1) * P], sx[:, n, k * KH:(k + 1) * KH], ident[:])
                ins.then_inc(s_xt, 1)

            def gate_up(n, e, parts):
                for q in parts:
                    for k in range(2):
                        ins = mm(ps[:, 3 * n + q, :], sx_t[n][:, k], gu_flat[:, bass.ds(e * (2 * 2 * FF) + (k * 2 * FF + q * 512), 512)],
                                 start=k == 0, stop=k == 1)
                return ins

            def hidden_transposes(j, n):
                pe.wait_ge(s_rh, j + 1)
                pe.wait_ge(s_rye, j + 1)
                for c in range(FC):
                    ins = nc.tensor.transpose(ps[:, 6 + c // 4, (c % 4) * P:(c % 4 + 1) * P], hid[:, n, c * P:(c + 1) * P], ident[:])
                ins.then_inc(s_ht, 1)

            def down(j, n, e):
                pe.wait_ge(s_hte, j + 1)
                for c in range(FC):
                    ins = mm(ps[:, 7, 256:256 + D], hid_t[n][:, c], dn_flat[:, bass.ds(e * (FC * D) + c * D, D)], start=c == 0, stop=c == FC - 1)
                ins.then_inc(s_ry, 1)

            def routed(j, n, e, e_before, loads):
                pe.wait_ge(s_xte, j + 1)
                gate_up(n, e, [0])
                hidden_transposes(j - 1, 1 - n)
                gate_up(n, e, [1, 2]).then_inc(s_rg, 1)
                if loads is not None:
                    slot_transposes(1 - n, loads)
                down(j - 1, 1 - n, e_before)

            slot_transposes(0, 1)
            e = expert_of(0)
            pe.wait_ge(s_xte, 1)
            gate_up(0, e, [0, 1, 2]).then_inc(s_rg, 1)
            slot_transposes(1, 1)
            with pe.Fori(0, SLOT_TILES // 2 - 1) as i:
                e = [expert_of(2 * i + n) for n in range(3)]
                for n in range(2):
                    routed(2 * i + 1 + n, 1 - n, e[n + 1], e[n], i + 2)
            last = SLOT_TILES - 1
            e = [expert_of(last - 1), expert_of(last)]
            routed(last, 1, e[1], e[0], None)
            hidden_transposes(last, 1)
            down(last, 1, e[1])

            pe.wait_ge(s_shw[1], 32)
            with pe.Fori(0, B) as b:
                pe.wait_ge(s_h, (B + 1 + b) * FC)
                shared_block(B + 1 + b, 1, bass.ds(b * SEQ, SEQ), SEQ, sh_h1)
            pe.wait_ge(s_h, (2 * B + 1) * FC)
            shared_block(2 * B + 1, 1, slice(NX, T), B, sh_h1)


def _layouts(i):
    f = i["L0_tok_freq_bands"]
    w = i["L0_tok_W"].reshape(D, VALS, 2, BANDS).transpose(1, 3, 2, 0)
    full = w[:XB * P].reshape(XB, P, BANDS, 2, D).transpose(1, 0, 2, 3, 4).reshape(P, XB * BANDS, 2, D)
    left = w[XB * P:].reshape(LEFT, BANDS // 2, 2, 2, D).transpose(2, 0, 1, 3, 4).reshape(P, BANDS // 2, 2, D)

    def gate_up(g, u):
        both = np.concatenate([g, u], axis=1)
        return both.transpose(0, 2, 1).reshape(len(g), 2, KH, 2 * FF).transpose(0, 2, 1, 3)

    def down(d):
        return d.transpose(0, 2, 1).reshape(len(d), FC, P, D).transpose(0, 2, 1, 3)

    channel = np.arange(INNER)
    heads = (channel[:, None] // DH == np.arange(NH)).astype(np.float32)
    return {
        "x_t": i["x"].reshape(NX, VALS).T,
        "freqs": np.concatenate([np.tile(f, (P, 1)), np.repeat(f.reshape(BANDS // 2, 2), LEFT, axis=1).T], axis=1),
        "w_tok": np.concatenate([full, left], axis=1),
        "cls4": np.tile(i["cls_tok"].reshape(1, D), (B, 1)),
        "w_qkv": i["L0_attn_w_qkv"].reshape(2, KH, INNER).transpose(1, 0, 2),
        "temp": i["L0_attn_temp"],
        "w_out": i["L0_attn_w_out"].reshape(CH, P, D).transpose(1, 0, 2),
        "b_out": np.tile(i["L0_attn_b_out"], (P, 1)),
        "gate_t": i["L0_ffn_gate_w"].T.reshape(2, KH, NE).transpose(1, 0, 2),
        "sh_gu": gate_up(i["L0_ffn_shared_gate"], i["L0_ffn_shared_up"]),
        "sh_dn": down(i["L0_ffn_shared_down"]),
        "ex_gu": gate_up(i["L0_ffn_routed_gate"], i["L0_ffn_routed_up"]),
        "ex_dn": down(i["L0_ffn_routed_down"]),
        "c_ident": np.eye(P, dtype=np.float32),
        "c_tri": np.triu(np.ones((P, P), np.float32), 1),
        "c_heads": heads.reshape(CH, P, NH).transpose(1, 0, 2),
        "c_spread": heads.T.reshape(NH, CH, P),
        "c_iota": np.tile(np.concatenate([np.arange(SLOT_TILES), np.arange(NE)]).astype(np.float32), (P, 1)),
        "c_valid": (np.arange(P)[:, None] < np.where(np.arange(NT) < CLS, P, B)).astype(np.float32),
    }


def kernel(**inputs):
    import concourse.bacc as bacc
    from concourse.bass_utils import run_bass_kernel_spmd

    nc = bacc.Bacc("TRN2", target_bir_lowering=False, num_devices=1)
    arrays = {k: np.ascontiguousarray(v) for k, v in _layouts({k: np.asarray(v) for k, v in inputs.items()}).items()}
    args = {k: nc.dram_tensor(k, v.shape, F32, kind="ExternalInput").ap() for k, v in arrays.items()}
    args["out"] = nc.dram_tensor("out", (B, SEQ + 1, D), F32, kind="ExternalOutput").ap()
    args["slots_x"] = nc.dram_tensor("slots_x", (SLOTS, D), F32).ap()
    args["slots_y"] = nc.dram_tensor("slots_y", (SLOTS, D), F32).ap()
    vit_tower(nc, **args)
    result = run_bass_kernel_spmd(nc, [arrays], core_ids=[0])
    return result.results[0]["out"]
```

```python
from contextlib import ExitStack, contextmanager

import numpy as np

import concourse.bass as bass
from concourse import mybir

F32 = mybir.dt.float32
F16 = mybir.dt.float16
F32R = mybir.dt.float32r
I32 = mybir.dt.int32
U32 = mybir.dt.uint32
ALU = mybir.AluOpType
ACT = mybir.ActivationFunctionType
AX_X = mybir.AxisListType.X

B, SEQ, D = 4, 512, 192
P = 128
NX = B * SEQ
NT = NX // P + 1
CLS = NT - 1
T = NX + B
TPB = SEQ // P
KH = D // 2
BANDS = 6
VALS = 3 * D
XB = VALS // P
LEFT = VALS - XB * P
STEPS = XB * BANDS + BANDS // 2
HALF = NX // 2
HT_ = HALF // P
NH, DH = 12, 64
INNER = NH * DH
CH = INNER // P
HPC = P // DH
NE, NS = 8, 2
FF = 768
FC = FF // P
SLOT_TILES = (2 * T - NE) // P + NE
SLOTS = SLOT_TILES * P
EPS = 1e-5
RING = 3
GU = 2 * 2 * FF
PIECE = 512
GU_PIECES = GU // PIECE
ROW = 2 * FF
X_UP = 4096.0
NORM_PIECES = 2 * (XB - 1) * BANDS
NORM = (NS + NE) * KH * GU // P // NORM_PIECES
COLS = 6


class Chain:

    def __init__(self, eng, sem):
        self.eng, self.sem, self.count, self.loops = eng, sem, 0, 0

    def __call__(self, ins):
        ins.then_inc(self.sem, 1)
        self.count += 1
        self.eng.wait_ge(self.sem, self.count + self.loops)

    @contextmanager
    def loop(self, trips, links):
        before = self.loops
        with self.eng.Fori(0, trips) as i:
            self.loops = before + i * links
            first = self.count
            yield i
            assert self.count == first + links, (self.count - first, links)
        self.loops = before
        self.count += links * (trips - 1)


def vit_tower(nc, x_t, freqs, w_tok, cls4, w_qkv, temp, w_out, b_out, gate_t, gu, sh_dn, ex_dn,
              c_ident, c_tri, c_heads, c_spread, c_iota, c_valid, out, slots_x, slots_y):
    ctx = ExitStack()
    base = -(-nc.sbuf_base // 32) * 32
    limit = nc.sbuf_base + nc.sbuf_bytes_remaining
    used = {}

    def at(name, shape, offset, dt=F32):
        size = -(-int(np.prod(shape[1:])) * (2 if dt == F16 else 4) // 32) * 32
        used[name] = nc.alloc_sbuf_tensor_at(name, shape, dt, offset=offset)
        assert offset + size <= limit, (name, offset + size, limit)
        return used[name], offset + size

    with ctx:
        o = base
        h_res, o = at("h_res", [P, NT, D], o)
        x16, _ = at("x16", [KH, 2, 2, T], o, F16)
        xn_t, o = at("xn_t", [KH, 2, T], o)
        ident, o = at("ident", [P, P], o)
        ones, o = at("ones", [P, P], o)
        tri, o = at("tri", [P, P], o)
        stats, o = at("stats", [P, NT, 6], o)
        mean_var, o = at("mean_var", [P, NT, 2], o)
        std, o = at("std", [P, NT], o)
        rstd, o = at("rstd", [P, NT], o)
        gate_sb, o = at("gate_sb", [KH, 2, NE], o)
        iota_sb, o = at("iota_sb", [P, SLOT_TILES + NE], o)
        valid_sb, o = at("valid_sb", [P, NT], o)
        before, _ = at("before", [1, SLOT_TILES, NE], o)
        place, _ = at("place", [P, NT, NE], o)
        logit, o = at("logit", [P, NT, NE], o)
        mask, _ = at("mask", [P, NT, NE], o)
        score, o = at("score", [P, NT, NE], o)
        top, o = at("top", [P, NT, 8], o)
        total, _ = at("total", [P, NT, NE], o)
        top_at, o = at("top_at", [P, NT, 8], o, U32)
        top_f, o = at("top_f", [P, NT, 8], o)
        pick = []
        for j in range(2):
            t_, o = at(f"pick{j}", [P, NT, NE], o)
            pick.append(t_)
        row, o = at("row", [P, 4, NT], o)
        weight, o = at("weight", [P, 2, NT], o)
        slot_f, o = at("slot_f", [P, NT], o)
        slot, o = at("slot", [P, 2, NT], o, I32)
        tiles_i, o = at("tiles_i", [P, NE], o, I32)
        tiles_f, o = at("tiles_f", [P, 3, NE], o)
        expert_f, o = at("expert_f", [1, SLOT_TILES], o)
        expert_i, o = at("expert_i", [1, SLOT_TILES], o, I32)
        half_pi, o = at("half_pi", [P, 1], o)
        eps_sb, o = at("eps_sb", [P, 1], o)
        peak, o = at("peak", [P, 2], o)
        root, o = at("root", [P, 1], o)
        w_up, o = at("w_up", [P, 1], o)
        gu_down, o = at("gu_down", [P, 1], o)
        experts_at = o
        pad_at = experts_at + NE * GU * 4
        down_at = pad_at + ROW * 4
        rest_at = down_at + NE * FC * D * 4

        o = experts_at
        x_sb, o = at("x_sb", [P, XB + 1, NX], o)
        feat = []
        for r in range(RING):
            t_, o = at(f"feat{r}", [P, 2, HALF], o)
            feat.append(t_)
        turns, o = at("turns", [P, HALF], o, I32)
        phase = []
        t_, phases_end = at("phase0", [P, 2, HALF], o)
        phase.append(t_)
        cols_sb, o = at("cols", [KH, COLS, 2, P], experts_at)
        w_sb, o = at("w_sb", [P, 2, CH, SEQ], o)
        w_cls, o = at("w_cls", [P, B, CH], o)
        w_sq, o = at("w_sq", [P, 2, CH, SEQ], o)
        w_cls_sq, o = at("w_cls_sq", [P, B, CH], o)
        wp, o = at("wp", [P, CH, SEQ + 1], o)
        scratch, o = at("scratch", [P, SEQ], o)
        w_out_b, o = at("w_out_b", [P, CH, D], o)
        norm_sq, o = at("norm_sq", [P, CH], o)
        inv_sq, o = at("inv_sq", [P, CH], o)
        norm_lhs, o = at("norm_lhs", [P, CH, NH], o)
        lg, o = at("lg", [NH, SEQ + 1], o)
        pi, o = at("pi", [NH, SEQ + 2], o)
        soft, o = at("soft", [NH, 4], o)
        dots, o = at("dots", [P, CH], o)
        cls_dots, o = at("cls_dots", [P, CH], o)
        neg_attn, o = at("neg_attn", [P, CH], o)
        wp_cls, o = at("wp_cls", [P, CH, B], o)
        o = max(o, phases_end)
        w_qkv_sb, o = at("w_qkv_sb", [KH, 2, INNER], o)
        w_out_sb, o = at("w_out_sb", [P, CH, D], o)
        heads_sb, o = at("heads_sb", [P, CH, NH], o)
        spread_sb, o = at("spread_sb", [NH, CH, P], o)
        temp_sb, o = at("temp_sb", [NH, 1], o)
        bias_sb, o = at("bias_sb", [P, D], o)
        pi_high, end = at("pi_high", [NH, SEQ], o, F32R)
        pi_low, end = at("pi_low", [NH, SEQ], end, F32R)
        spread_r, end = at("spread_r", [NH, CH, P], end, F32R)
        assert end <= down_at
        for r in range(1, RING):
            t_, o = at(f"phase{r}", [P, 2, HALF], o)
            phase.append(t_)
        w_tok_sb, o = at("w_tok_sb", [P, STEPS, 2, D], o)
        freq_sb, o = at("freq_sb", [P, BANDS + BANDS // 2], o)
        stage, o = at("stage", [P, 2, NORM], o)
        weight_norms, o = at("weight_norms", [P, NORM_PIECES], o)
        assert o <= limit - NT * D * 4

        ex16 = nc.alloc_sbuf_tensor_at("ex16", [KH, NE * GU * 2], F16, offset=experts_at)
        ex_raw = nc.alloc_sbuf_tensor_at("ex_raw", [KH, NE, 2, 2 * FF], F32, offset=experts_at + ROW * 4)
        ex_dn_sb, o = at("ex_dn_sb", [P, NE, FC, D], down_at)
        assert o == rest_at
        xn_at = (limit - NT * D * 4) // 32 * 32
        xn, _ = at("xn", [P, NT, D], xn_at)
        zeros, _ = at("zeros", [P, 4, D], xn_at)
        sh_dn_sb, sh16, sh_raw = [], [], []
        for i in range(NS):
            t_, o = at(f"sh_dn{i}", [P, FC, D], rest_at)
            sh_dn_sb.append(t_)
            sh_raw.append(at(f"sh_raw{i}", [KH, 2, 2 * FF], o + PIECE * 4)[0])
            t_, o = at(f"sh16_{i}", [KH, GU_PIECES, 2, PIECE], o, F16)
            sh16.append(t_)
        shared_end = o
        sh_h, o = at("sh_h", [P, 2, SEQ], o)
        assert max(o, shared_end + PIECE * 4) <= xn_at
        o = xn_at
        sx, o = at("sx", [P, 2, D], o)
        sx_t = [None, None]
        sx_t[0], o = at("sx_t0", [KH, 2, 2, P], o, F16)
        sx_t[1], o = at("sx_t1", [KH, 2, 2, P], o, F16)
        hid, o = at("hid", [P, 2, FF], o)
        sy, o = at("sy", [P, 2, D], o)
        o = pad_at
        hid_t = [None, None]
        hid_t[0], o = at("hid_t0", [P, FC, P], o)
        hid_t[1], o = at("hid_t1", [P, FC, P], o)
        assert o <= down_at
        o = experts_at
        sh_h1, o = at("sh_h1", [P, 2, SEQ], o)
        gat, o = at("gat", [P, 2, NT, D], o)

        ps = ctx.enter_context(nc.psum_tensor("ps", [P, 8, 512], F32))

        def sem(name):
            return ctx.enter_context(nc.semaphore(name))

        s_const = sem("constants_loaded")
        s_x = [sem(f"x_{name}_loaded") for name in ("first_block", "half0", "half1")]
        s_wtok = [sem(f"w_tok_{name}_loaded") for name in ("first_step", "first_block", "rest")]
        s_freq = sem("frequencies_loaded")
        s_cls = sem("class_tokens_loaded")
        s_attnw = sem("attention_weights_loaded")
        s_zero = sem("zeros_ready")
        s_own = sem("vector_constants_ready")
        s_zeroed = sem("slots_zeroed")
        s_turns = sem("phases_ready")
        s_feat = sem("features_ready")
        s_used = sem("features_used")
        s_hrow = sem("token_rows_evacuated")
        s_dchain = sem("vector_chain")
        s_var = sem("variances_ready")
        s_std = sem("deviations_ready")
        s_xn = sem("normalised_ready")
        s_xnp = sem("normalised_transposed")
        s_xnt = sem("normalised_columns_ready")
        s_hb = sem("bias_added")
        s_q = sem("projection_ready")
        s_qe = sem("projection_evacuated")
        s_qcls = sem("class_projection_ready")
        s_nl = sem("norm_weights_ready")
        s_lg = sem("logits_ready")
        s_mx = sem("logit_maximum_ready")
        s_exp = sem("attention_exp_ready")
        s_pi = sem("pi_ready")
        s_pisum = sem("pi_sum_ready")
        s_wcls = sem("class_projection_evacuated")
        s_pb = sem("pi_spread")
        s_pbe = sem("pi_spread_used")
        s_wo = sem("scaled_w_out_ready")
        s_y = sem("attention_out_ready")
        s_ye = sem("attention_out_added")
        s_stage = [sem(f"weights_staged{i}") for i in range(2)]
        s_norm = sem("weight_norms_taken")
        s_peak = sem("weight_peak_ready")
        s_peakt = sem("weight_peak_moved")
        s_root = sem("weight_root_ready")
        s_xl = sem("low_columns_ready")
        s_split = [sem(f"shared{i}_weights_split") for i in range(NS)]
        s_exhigh = sem("expert_high_parts_ready")
        s_exlow = sem("expert_low_parts_ready")
        s_rl = sem("router_logits_ready")
        s_re1 = sem("early_router_logits_copied")
        s_rm = sem("router_maximum_taken")
        s_re = sem("router_exp_ready")
        s_mask = sem("mask_ready")
        s_cnt = sem("counts_ready")
        s_slot = sem("slots_ready")
        s_te = sem("tile_experts_ready")
        s_scat = sem("rows_scattered")
        s_shw = [sem(f"shared{i}_weights_loaded") for i in range(2)]
        s_exw = sem("expert_gate_up_loaded")
        s_exd = sem("expert_down_loaded")
        s_gu = sem("shared_gate_up_ready")
        s_silu = sem("shared_silu_ready")
        s_h = sem("shared_hidden_ready")
        s_dn = sem("shared_hidden_used")
        s_ya = sem("shared_out_added")
        s_sxe = [sem(f"slot_rows_loaded{i}") for i in range(2)]
        s_xt = sem("slot_rows_transposed")
        s_xte = sem("slot_columns_ready")
        s_rg = sem("routed_gate_up_ready")
        s_rs = sem("routed_silu_ready")
        s_rh = sem("routed_hidden_ready")
        s_ht = sem("routed_hidden_transposed")
        s_hte = sem("routed_hidden_columns_ready")
        s_ry = sem("routed_out_ready")
        s_rye = sem("routed_out_evacuated")
        s_rst = [sem(f"routed_out_stored{i}") for i in range(2)]
        s_gat = [sem(f"rows_gathered{b}") for b in range(B + 1)]
        s_out = sem("out_stored")

        block = ctx.enter_context(nc.Block())

        def tile_rows(t):
            return P if t < CLS else B

        def columns(t):
            return slice(t * P, t * P + tile_rows(t))

        def tiles_of(group, last):
            own = [group * TPB + t for t in range(TPB)]
            return own + [CLS] if group == (B - 1 if last else 0) else own

        def order(n, group):
            return group * TPB + (group > 0 and n == 0)

        def bank(n, group, j):
            if n == 0:
                return 4 + (order(0, group) + j) % 4
            return 6 if group > 0 else j % 2

        def transposed_at_once(n, group):
            return 4 if n == 0 else 1 if group > 0 else 2

        slots_of = [(0, 0), (0, 1)] + [(c, place_) for c in range(1, FC) for place_ in range(3)]
        BETWEEN = {slot_: TPB + n for n, slot_ in enumerate(slots_of[:NT - TPB])}
        EARLY = TPB
        CLASS_UNIT = B * FC

        PIECES, FIRST = 2 * NE - (B - 2) * FC, 1

        def unit(s, b, c):
            return s * (CLASS_UNIT + 1) + b * FC + c

        def y_tile(t, r=P):
            return ps[0:r, 4 + t // 2, (t % 2) * D:(t % 2 + 1) * D]

        @block.sync
        def _(sp):
            def load_x(blocks, cols, done):
                for c in blocks:
                    if c < XB:
                        sp.dma_start(x_sb[:, c, cols], x_t[c * P:(c + 1) * P, cols]).then_inc(done, 16)
                    else:
                        for part in range(P // LEFT):
                            sp.dma_start(x_sb[part * LEFT:(part + 1) * LEFT, XB, cols], x_t[XB * P:, cols]).then_inc(done, 16)

            sp.dma_start(freq_sb[:], freqs).then_inc(s_freq, 16)
            load_x([0], slice(0, HALF), s_x[0])
            load_x(range(1, XB + 1), slice(0, HALF), s_x[1])
            gu_flat = gu.rearrange("e k a n -> (e k a n)").rearrange("(p n) -> p n", p=P)
            for n in range(2):
                sp.dma_start(stage[:, n], gu_flat[:, n * NORM:(n + 1) * NORM]).then_inc(s_stage[n], 16)
            load_x(range(XB + 1), slice(HALF, NX), s_x[2])
            sp.dma_start(ident[:], c_ident).then_inc(s_const, 16)
            sp.dma_start(h_res[0:B, CLS, :], cls4).then_inc(s_cls, 16)
            sp.dma_start(tri[:], c_tri).then_inc(s_const, 16)
            sp.dma_start(gate_sb[:], gate_t).then_inc(s_const, 16)
            sp.dma_start(iota_sb[:], c_iota).then_inc(s_const, 16)
            sp.dma_start(valid_sb[:], c_valid).then_inc(s_const, 16)
            sp.dma_start(w_qkv_sb[:], w_qkv).then_inc(s_attnw, 16)
            sp.dma_start(w_out_sb[:], w_out).then_inc(s_attnw, 16)
            sp.dma_start(heads_sb[:], c_heads).then_inc(s_attnw, 16)
            sp.dma_start(spread_sb[:], c_spread).then_inc(s_attnw, 16)
            sp.dma_start(temp_sb[:], temp).then_inc(s_attnw, 16)
            sp.dma_start(bias_sb[:], b_out).then_inc(s_attnw, 16)
            sp.wait_ge(s_zero, 1)
            zero_rows = slots_x.rearrange("(n a p) d -> n p a d", p=P, a=4)
            for n in range(SLOT_TILES // 4):
                sp.dma_start(zero_rows[n], zeros[:]).then_inc(s_zeroed, 16)
            with sp.Fori(1, NORM_PIECES // 2) as i:
                for n in range(2):
                    sp.wait_ge(s_norm, 2 * i + n - 1)
                    sp.dma_start(stage[:, n], gu_flat[:, bass.ds((2 * i + n) * NORM, NORM)]).then_inc(s_stage[n], 16)
            sp.wait_ge(s_used, 2 * STEPS + RING)
            sp.wait_ge(s_peak, 1)
            sp.dma_start(sh_raw[0][:], gu[0]).then_inc(s_shw[0], 16)
            sp.dma_start(sh_dn_sb[0][:], sh_dn[0]).then_inc(s_shw[0], 16)
            for e in range(NE):
                sp.dma_start(ex_dn_sb[:, e], ex_dn[e]).then_inc(s_exd, 16)
            sp.wait_ge(s_ye, B + 2)
            for e in range(NE):
                sp.dma_start(ex_raw[:, e], gu[NS + e]).then_inc(s_exw, 16)
            sp.wait_ge(s_scat, 16 * 2 * NT)
            for n in range(2):
                sp.dma_start(sx[:, n], slots_x[n * P:(n + 1) * P, :]).then_inc(s_sxe[n], 16)
            sp.wait_ge(s_ya, B + 2)
            sp.dma_start(sh_raw[1][:], gu[1]).then_inc(s_shw[1], 16)
            sp.dma_start(sh_dn_sb[1][:], sh_dn[1]).then_inc(s_shw[1], 16)
            with sp.Fori(0, SLOT_TILES // 2 - 1) as i:
                for n in range(2):
                    sp.wait_ge(s_xt, 2 * i + n + 1)
                    sp.dma_start(sx[:, n], slots_x[bass.ds((2 * i + 2 + n) * P, P), :]).then_inc(s_sxe[n], 16)
            for b in range(B):
                sp.wait_ge(s_ya, (B + 2) + b + 1)
                sp.dma_start(out[b, 1:, :].rearrange("(t p) d -> p t d", p=P), h_res[:, b * TPB:(b + 1) * TPB, :]).then_inc(s_out, 16)
            sp.wait_ge(s_ya, 2 * (B + 1) + 1)
            sp.dma_start(out[:, 0, :], h_res[0:B, CLS, :]).then_inc(s_out, 16)
            sp.wait_ge(s_out, 16 * (B + 1))

        @block.gpsimd
        def _(pool):
            nc.gpsimd.memset(zeros[:], 0.0).then_inc(s_zero, 1)
            pool.wait_ge(s_attnw, 16 * 6)
            for g in range(B):
                pool.wait_ge(s_xn, g + 1)
                for t in tiles_of(g, False):
                    r = tile_rows(t)
                    nc.gpsimd.tensor_tensor(h_res[0:r, t], h_res[0:r, t], bias_sb[0:r, :], ALU.add).then_inc(s_hb, 1)
            for g in range(B):
                for j, t in enumerate(tiles_of(g, True)):
                    at_, r = order(1, g) + j, tile_rows(t)
                    pool.wait_ge(s_xnt, NT + at_ + 1)
                    nc.gpsimd.tensor_tensor(x16[:, 1, :, columns(t)], cols_sb[:, at_ % COLS, :, 0:r], x16[:, 0, :, columns(t)],
                                            ALU.subtract).then_inc(s_xl, 1)
            pool.wait_ge(s_slot, 2)
            pool.wait_ge(s_zeroed, 16 * (SLOT_TILES // 4))
            for t in range(NT):
                r = tile_rows(t)
                for j in range(2):
                    nc.gpsimd.indirect_dma_start(
                        slots_x, bass.IndirectOffsetOnAxis(ap=slot[0:r, j, t:t + 1], axis=0),
                        xn[0:r, t, :], None).then_inc(s_scat, 16)
            pool.wait_ge(s_shw[1], 32)
            flat_raw = sh_raw[1][:].rearrange("p k n -> p (k n)")
            for p in range(GU_PIECES):
                raw, (high, low) = flat_raw[:, p * PIECE:(p + 1) * PIECE], (sh16[1][:, p, 0], sh16[1][:, p, 1])
                nc.gpsimd.tensor_scalar(raw, raw, w_up[0:KH], None, ALU.mult).then_inc(s_split[1], 1)
                pool.wait_ge(s_split[1], 3 * p + 1)
                nc.gpsimd.tensor_copy(high, raw).then_inc(s_split[1], 1)
                pool.wait_ge(s_split[1], 3 * p + 2)
                nc.gpsimd.tensor_tensor(low, raw, high, ALU.subtract).then_inc(s_split[1], 1)
                pool.wait_ge(s_split[1], 3 * p + 3)

            for n in range(2):
                pool.wait_ge(s_rst[n], 16 * (SLOT_TILES // 2))
            pool.wait_ge(s_ry, SLOT_TILES)
            for t in range(NT):
                r = tile_rows(t)
                for j in range(2):
                    nc.gpsimd.indirect_dma_start(
                        gat[0:r, j, t, :], None, slots_y,
                        bass.IndirectOffsetOnAxis(ap=slot[0:r, j, t:t + 1], axis=0)).then_inc(s_gat[t // TPB], 16)

        @block.scalar
        def _(act):
            flat = w_tok_sb[:].rearrange("p s a d -> p (s a d)")
            flat_in = w_tok.rearrange("p s a d -> p (s a d)")
            ends = [0, 2 * D, BANDS * 2 * D, STEPS * 2 * D]
            for done, start, end in zip(s_wtok, ends, ends[1:]):
                act.dma_start(flat[:, start:end], flat_in[:, start:end]).then_inc(done, 16)
            act.wait_ge(s_own, 1)
            nc.scalar.activation(root[:], half_pi[:], ACT.Sin)

            def sines(step, r):
                act.wait_ge(s_turns, 2 * step + 2)
                act.wait_ge(s_used, step + 1)
                nc.scalar.activation(feat[r][:, 0], phase[r][:, 0], ACT.Sin, scale=6.283185).then_inc(s_feat, 1)
                nc.scalar.activation(feat[r][:, 1], phase[r][:, 1], ACT.Sin, bias=half_pi[:], scale=-6.283185).then_inc(s_feat, 1)

            def norm_piece(c, k, half):
                piece = half * (XB - 1) * BANDS + (c - 1) * BANDS + k
                act.wait_ge(s_stage[k % 2], 16 * (half * (XB - 1) * BANDS // 2 + (c - 1) * (BANDS // 2) + k // 2 + 1))
                nc.scalar.activation(stage[:, k % 2], stage[:, k % 2], ACT.Square, accum_out=weight_norms[:, bass.ds(piece, 1)]).then_inc(s_norm, 1)

            def deviations(n, group):
                act.wait_ge(s_var, n * B + group + 1)
                first, own = group * TPB, tiles_of(group, n == 1)
                ins = nc.scalar.activation(std[:, first:first + TPB], mean_var[:, first:first + TPB, 1], ACT.Sqrt, bias=eps_sb[:])
                if CLS in own:
                    ins = nc.scalar.activation(std[0:B, CLS:CLS + 1], mean_var[0:B, CLS, 1:2], ACT.Sqrt, bias=eps_sb[0:B])
                ins.then_inc(s_std, 1)

            def norm_columns(n, group, part=slice(None)):
                for j, t in list(enumerate(tiles_of(group, n == 1)))[part]:
                    r = tile_rows(t)
                    act.wait_ge(s_xnp, n * NT + order(n, group) + j + 1)
                    moved = ps[0:KH, bank(n, group, j), 0:2 * r].rearrange("p (k n) -> p k n", k=2)
                    if n == 0:
                        nc.scalar.copy(xn_t[:, :, columns(t)], moved).then_inc(s_xnt, 1)
                        continue
                    at_ = order(n, group) + j
                    if at_ >= COLS:
                        act.wait_ge(s_xl, at_ - COLS + 1)
                        act.wait_ge(s_rl, at_ - COLS + 1)
                    nc.scalar.mul(cols_sb[:, at_ % COLS, :, 0:r], moved, X_UP)
                    nc.scalar.mul(x16[:, 0, :, columns(t)], moved, X_UP).then_inc(s_xnt, 1)

            def attention_columns(b):
                for c in range(CH):
                    act.wait_ge(s_q, b * CH + c + 1)
                    nc.scalar.copy(w_sb[:, bass.ds(b % 2, 1), c], ps[:, c % 2:c % 2 + 1, :])
                    nc.scalar.activation(w_sq[:, bass.ds(b % 2, 1), c], ps[:, c % 2:c % 2 + 1, :], ACT.Square,
                                         accum_out=norm_sq[:, c:c + 1]).then_inc(s_qe, 1)

            def exponentials(b):
                act.wait_ge(s_mx, b + 1)
                nc.scalar.activation(pi[:, 0:SEQ + 1], lg[:], ACT.Exp, bias=soft[:, 0:1], accum_out=soft[:, 1:2]).then_inc(s_exp, 1)

            for half in range(2):
                for k in range(half, BANDS):
                    sines(half * STEPS + k, k % RING)
                if half:
                    deviations(0, 0)
                    deviations(0, 1)
                with act.Fori(1, XB) as c:
                    for k in range(BANDS):
                        sines(half * STEPS + c * BANDS + k, k % RING)
                        norm_piece(c, k, half)
                for k in range(BANDS // 2):
                    sines(half * STEPS + XB * BANDS + k, k % RING)
                if half == 0:
                    sines(STEPS, 0)
                act.wait_ge(s_used, half * STEPS + STEPS + RING)
                for j in range(HT_) if half == 0 else [*range(HT_ - 4, HT_), *range(HT_ - 4)]:
                    nc.scalar.copy(h_res[:, half * HT_ + j, :], ps[:, j, 0:D]).then_inc(s_hrow, 1)
            norm_columns(0, 0)
            deviations(0, 2)
            deviations(0, 3)
            act.wait_ge(s_peakt, 2)
            nc.scalar.activation(root[:], ps[:, 3, P:P + 1], ACT.Sqrt).then_inc(s_root, 1)
            act.wait_ge(s_qcls, 1)
            by_chunk = ps[:, 2, 0:CH * B].rearrange("p (c b) -> p b c", b=B)
            nc.scalar.copy(w_cls[:], by_chunk)
            nc.scalar.activation(w_cls_sq[:], by_chunk, ACT.Square).then_inc(s_wcls, 1)
            attention_columns(0)
            norm_columns(0, 1)
            norm_columns(0, 2)
            norm_columns(0, 3)
            exponentials(0)
            with act.Fori(0, B - 1) as b:
                attention_columns(b + 1)
                exponentials(b + 1)
            for g in range(B - 1):
                deviations(1, g)
            norm_columns(1, 0)

            def norm_columns_between(c, place_):
                if (c, place_) in BETWEEN:
                    t = BETWEEN[c, place_]
                    group = min(t // TPB, B - 1)
                    norm_columns(1, group, slice(t - group * TPB, t - group * TPB + 1))

            def silu_chunk(u, c, hidden):
                act.wait_ge(s_gu, u + 1)
                act.wait_ge(s_dn, u + 1)
                nc.scalar.activation(hidden[:, c % 2], ps[:, 2 * (c % 2), :], ACT.Silu, scale=gu_down[:]).then_inc(s_silu, 1)

            def silu_class(u, hidden):
                act.wait_ge(s_gu, u + 1)
                act.wait_ge(s_dn, u + 1)
                nc.scalar.activation(hidden[:, 0, 0:FC * B], ps[:, 6, 0:FC * B], ACT.Silu, scale=gu_down[:]).then_inc(s_silu, 1)

            raw_flat = ex_raw[:].rearrange("p e k n -> p (e k n)")

            def high_part(p):
                act.wait_ge(s_exlow, p)
                nc.scalar.activation(ex16[:, bass.ds(p * (2 * ROW), ROW)], raw_flat[:, bass.ds(p * ROW, ROW)], ACT.Copy,
                                     scale=w_up[0:KH]).then_inc(s_exhigh, 1)

            for c in range(FC):
                norm_columns_between(c, 0)
                if c == 0:
                    deviations(1, B - 1)
                silu_chunk(unit(0, 0, c), c, sh_h)
                norm_columns_between(c, 1)
                norm_columns_between(c, 2)
            act.wait_ge(s_rm, 1)
            nc.scalar.activation(score[:], logit[:], ACT.Exp, scale=1.0 / X_UP).then_inc(s_re, 1)
            for c in range(FC):
                if c == FIRST:
                    act.wait_ge(s_exw, 16 * NE)
                if FIRST <= c < FIRST + PIECES:
                    high_part(c - FIRST)
                silu_chunk(unit(0, 1, c), c, sh_h)
            with act.Fori(2, B) as b:
                for c in range(FC):
                    high_part(PIECES + (b - 2) * FC + c)
                    silu_chunk(unit(0, b, c), c, sh_h)
            silu_class(CLASS_UNIT, sh_h)

            def silu(j, n):
                act.wait_ge(s_rg, j + 1)
                nc.scalar.activation(hid[:, n, :], ps[:, 3 * n:3 * n + 3, :].rearrange("p a n -> p (a n)")[:, 0:FF], ACT.Silu,
                                     scale=gu_down[:]).then_inc(s_rs, 1)

            def hidden_columns(j, n):
                act.wait_ge(s_ht, j + 1)
                nc.scalar.copy(hid_t[n][:], ps[:, 6:8, :].rearrange("p a n -> p (a n)")[:, 0:FF].rearrange("p (c n) -> p c n", c=FC)).then_inc(s_hte, 1)

            def store(j, n):
                act.wait_ge(s_rye, j + 2)
                act.dma_start(slots_y[bass.ds(j * P, P), :], sy[:, n]).then_inc(s_rst[n], 16)

            silu(0, 0)
            hidden_columns(0, 0)
            silu(1, 1)
            store(0, 0)
            with act.Fori(1, SLOT_TILES // 2) as i:
                for n in range(2):
                    hidden_columns(2 * i + n - 1, 1 - n)
                    silu(2 * i + n, n)
                    store(2 * i + n - 1, 1 - n)
            hidden_columns(SLOT_TILES - 1, 1)
            store(SLOT_TILES - 1, 1)
            act.wait_ge(s_rg, SLOT_TILES)
            with act.Fori(0, B) as b:
                for c in range(FC):
                    silu_chunk(unit(1, b, c), c, sh_h1)
            silu_class(unit(1, B, 0), sh_h1)

        @block.vector
        def _(dve):
            link = Chain(dve, s_dchain)
            nc.vector.memset(half_pi[:], float(np.pi / 2))
            nc.vector.memset(eps_sb[:], EPS)
            nc.vector.memset(ones[:], 1.0).then_inc(s_used, RING)
            nc.vector.memset(std[:], 1.0).then_inc(s_feat, 2 * RING)
            nc.vector.memset(rstd[:], 1.0).then_inc(s_ye, 1)
            nc.vector.memset(score[:], 0.0).then_inc(s_ya, 1)
            nc.vector.memset(top[:], 0.0).then_inc(s_rye, 1)
            nc.vector.memset(logit[:], 0.0).then_inc(s_dn, 2)
            nc.vector.memset(mean_var[:], 1.0).then_inc(s_own, 1)
            dve.wait_ge(s_own, 1)

            def phases(step, r, x, f):
                link(nc.vector.tensor_scalar(turns[:], x, freq_sb[:, f:f + 1], None, ALU.mult))
                dve.wait_ge(s_feat, 2 * step + 2)
                nc.vector.scalar_tensor_tensor(out=phase[r][:, 0], in0=x, scalar=freq_sb[:, f:f + 1], in1=turns[:],
                                               op0=ALU.mult, op1=ALU.subtract).then_inc(s_turns, 1)
                dve.wait_ge(s_turns, 2 * step + 1)
                nc.vector.tensor_scalar(phase[r][:, 1].bitcast(I32), phase[r][:, 0].bitcast(I32), 0x7FFFFFFF, None,
                                        ALU.bitwise_and).then_inc(s_turns, 1)

            def deviation_inputs(n, group):
                own = tiles_of(group, n == 1)
                for t in own:
                    if n == 0 or t == CLS:
                        r = tile_rows(t)
                        last = nc.vector.bn_stats(stats[0:r, t], h_res[0:r, t, :])
                if n == 0 or CLS in own:
                    link(last)
                for t in own:
                    r = tile_rows(t)
                    last = nc.vector.bn_aggr(mean_var[0:r, t], stats[0:r, t])
                last.then_inc(s_var, 1)

            def normalise(n, group):
                own = tiles_of(group, n == 1)
                dve.wait_ge(s_std, n * B + group + 1)
                first = group * TPB
                if CLS in own:
                    nc.vector.reciprocal(rstd[0:B, CLS:CLS + 1], std[0:B, CLS:CLS + 1])
                link(nc.vector.reciprocal(rstd[:, first:first + TPB], std[:, first:first + TPB]))
                for t in own:
                    r = tile_rows(t)
                    last = nc.vector.tensor_scalar(xn[0:r, t], h_res[0:r, t, :], mean_var[0:r, t, 0:1], rstd[0:r, t:t + 1],
                                                   ALU.subtract, ALU.mult)
                last.then_inc(s_xn, 1)

            dve.wait_ge(s_freq, 16)
            for half in range(2):
                cols = slice(half * HALF, (half + 1) * HALF)
                dve.wait_ge(s_x[2 * half], 16 if half == 0 else 16 * (XB + 2))
                for k in range(BANDS):
                    phases(half * STEPS + k, k % RING, x_sb[:, 0, cols], k)
                if half:
                    dve.wait_ge(s_hrow, HT_)
                    dve.wait_ge(s_cls, 16)
                    deviation_inputs(0, 0)
                    deviation_inputs(0, 1)
                else:
                    dve.wait_ge(s_x[1], 16 * (XB + 1))
                with link.loop(XB - 1, BANDS) as i:
                    for k in range(BANDS):
                        phases(half * STEPS + (i + 1) * BANDS + k, k % RING, x_sb[:, bass.ds(i + 1, 1), cols].rearrange("p a n -> p (a n)"), k)
                if half:
                    dve.wait_ge(s_zeroed, 16 * (SLOT_TILES // 4))
                    normalise(0, 0)
                    normalise(0, 1)
                for k in range(BANDS // 2):
                    phases(half * STEPS + XB * BANDS + k, k % RING, x_sb[:, XB, cols], BANDS + k)
            dve.wait_ge(s_norm, NORM_PIECES)
            nc.vector.tensor_reduce(peak[:, 0:1], weight_norms[:], AX_X, ALU.max).then_inc(s_peak, 1)
            dve.wait_ge(s_hrow, CLS)
            deviation_inputs(0, 2)
            dve.wait_ge(s_peakt, 1)
            link(nc.vector.tensor_reduce(peak[0:1, 1:2], ps[0:1, 3, 0:P], AX_X, ALU.max))
            nc.vector.tensor_scalar(peak[0:1, 1:2], peak[0:1, 1:2], 1e-30, None, ALU.max).then_inc(s_peak, 1)
            deviation_inputs(0, 3)
            normalise(0, 2)
            normalise(0, 3)
            dve.wait_ge(s_root, 1)
            link(nc.vector.tensor_scalar(root[:].bitcast(I32), root[:].bitcast(I32), 0x7F800000, None, ALU.bitwise_and))
            link(nc.vector.tensor_scalar(gu_down[:], root[:], 2.0 ** -14 / X_UP, None, ALU.mult))
            link(nc.vector.reciprocal(w_up[:], root[:]))
            link(nc.vector.tensor_scalar(w_up[:], w_up[:], 2.0 ** 14, None, ALU.mult))
            dve.wait_ge(s_attnw, 16 * 6)

            def norms(b):
                dve.wait_ge(s_qe, (b + 1) * CH)
                link(nc.vector.tensor_tensor(norm_sq[:], norm_sq[:], w_cls_sq[:, bass.ds(b, 1)].rearrange("p a c -> p (a c)"), ALU.add))
                link(nc.vector.tensor_scalar(norm_sq[:], norm_sq[:], 1e-24, None, ALU.max))
                link(nc.vector.reciprocal(inv_sq[:], norm_sq[:]))
                nc.vector.tensor_tensor(norm_lhs[:], heads_sb[:], inv_sq[:].rearrange("p (c a) -> p c a", a=1).to_broadcast([P, CH, NH]),
                                        ALU.mult).then_inc(s_nl, 1)

            def softmax(b):
                dve.wait_ge(s_lg, b + 1)
                nc.vector.tensor_scalar(lg[:, 0:SEQ], ps[0:NH, 3, :], temp_sb[:], None, ALU.mult)
                link(nc.vector.tensor_scalar(lg[:, SEQ:SEQ + 1], ps[0:NH, 2, 32:33], temp_sb[:], None, ALU.mult))
                nc.vector.tensor_reduce(soft[:, 0:1], lg[:], AX_X, ALU.max, negate=True).then_inc(s_mx, 1)
                dve.wait_ge(s_exp, b + 1)
                link(nc.vector.reciprocal(soft[:, 2:3], soft[:, 1:2]))
                link(nc.vector.tensor_scalar(pi[:, 0:SEQ + 1], pi[:, 0:SEQ + 1], soft[:, 2:3], None, ALU.mult))
                link(nc.vector.tensor_copy(pi_high[:], pi[:, 0:SEQ]))
                nc.vector.tensor_tensor(pi_low[:], pi[:, 0:SEQ], pi_high[:], ALU.subtract).then_inc(s_pi, 1)
                link(nc.vector.tensor_reduce(soft[:, 3:4], pi[:, 0:SEQ + 1], AX_X, ALU.add))
                link(nc.vector.tensor_scalar(soft[:, 3:4], soft[:, 3:4], 1e-8, None, ALU.add))
                nc.vector.reciprocal(pi[:, SEQ + 1:SEQ + 2], soft[:, 3:4]).then_inc(s_pisum, 1)

            def w_by_pi(b, chunks):
                w = w_sb[:, bass.ds(b % 2, 1)].rearrange("p a c n -> p (a c) n")
                for c in chunks:
                    dve.wait_ge(s_pb, b * (CH + 1) + c + 1)
                    link(nc.vector.tensor_tensor(wp[:, c, 0:SEQ], ps[:, 6 + c % 2, :], w[:, c], ALU.mult))
                    nc.vector.scalar_tensor_tensor(out=scratch[:], in0=wp[:, c, 0:SEQ], scalar=1.0, in1=w[:, c],
                                                   op0=ALU.mult, op1=ALU.mult, accum_out=dots[:, c:c + 1]).then_inc(s_pbe, 1)

            def scale_w_out(b):
                w_class = w_cls[:, bass.ds(b, 1)].rearrange("p a c -> p (a c)")
                spread = ps[:, 2, P:P + 2 * CH].rearrange("p (c a) -> p c a", a=2)
                dve.wait_ge(s_pb, (b + 1) * (CH + 1))
                link(nc.vector.tensor_tensor(wp[:, :, SEQ], spread[:, :, 0], w_class, ALU.mult))
                link(nc.vector.tensor_tensor(cls_dots[:], wp[:, :, SEQ], w_class, ALU.mult))
                dve.wait_ge(s_pbe, b * CH + CH)
                link(nc.vector.tensor_tensor(dots[:], dots[:], cls_dots[:], ALU.add))
                link(nc.vector.tensor_tensor(dots[:], dots[:], spread[:, :, 1], ALU.mult))
                link(nc.vector.tensor_scalar(dots[:], dots[:], 1.0, -1.0, ALU.add, ALU.mult))
                nc.vector.reciprocal(neg_attn[:], dots[:]).then_inc(s_wo, 1)
                dve.wait_ge(s_wo, 2 * b + 1)
                nc.vector.tensor_tensor(wp_cls[:, :, bass.ds(b, 1)].rearrange("p c a -> p (c a)"), wp[:, :, SEQ], neg_attn[:], ALU.mult)
                nc.vector.tensor_tensor(w_out_b[:], w_out_sb[:], neg_attn[:].rearrange("p (c a) -> p c a", a=1).to_broadcast([P, CH, D]),
                                        ALU.mult).then_inc(s_wo, 1)

            def attended(b):
                dve.wait_ge(s_y, b + 1)
                for t in range(TPB):
                    last = nc.vector.tensor_tensor(h_res[:, bass.ds(b * TPB + t, 1), :], y_tile(t).rearrange("p (a d) -> p a d", a=1),
                                                   h_res[:, bass.ds(b * TPB + t, 1), :], ALU.add)
                last.then_inc(s_ye, 1)
                dve.wait_ge(s_ye, b + 2)
                for t in range(TPB):
                    last = nc.vector.bn_stats(stats[:, bass.ds(b * TPB + t, 1)].rearrange("p a s -> p (a s)"),
                                              h_res[:, bass.ds(b * TPB + t, 1), :].rearrange("p a d -> p (a d)"))
                link(last)

            dve.wait_ge(s_hb, NT)
            link(nc.vector.tensor_copy(spread_r[:], spread_sb[:]))
            dve.wait_ge(s_wcls, 1)
            norms(0)
            dve.wait_ge(s_shw[0], 32)
            flat_raw = sh_raw[0][:].rearrange("p k n -> p (k n)")
            for p in range(GU_PIECES):
                raw, (high, low) = flat_raw[:, p * PIECE:(p + 1) * PIECE], (sh16[0][:, p, 0], sh16[0][:, p, 1])
                link(nc.vector.tensor_scalar(high, raw, w_up[0:KH], None, ALU.mult))
                last = nc.vector.scalar_tensor_tensor(out=low, in0=raw, scalar=w_up[0:KH], in1=high, op0=ALU.mult, op1=ALU.subtract)
                if p < GU_PIECES - 1:
                    link(last)
            last.then_inc(s_split[0], 1)
            softmax(0)
            with link.loop(B - 1, 20 + 1) as b:
                w_by_pi(b, range(CH))
                norms(b + 1)
                scale_w_out(b)
                softmax(b + 1)
                attended(b)
            for g in range(B - 1):
                deviation_inputs(1, g)
            w_by_pi(B - 1, [0])
            normalise(1, 0)
            w_by_pi(B - 1, range(1, CH))
            scale_w_out(B - 1)
            for g in range(1, B - 1):
                normalise(1, g)
            dve.wait_ge(s_rl, EARLY)
            nc.vector.tensor_copy(logit[:, 0:EARLY], ps[:, 3, 0:EARLY * NE].rearrange("p (t e) -> p t e", e=NE)).then_inc(s_re1, 1)
            attended(B - 1)
            dve.wait_ge(s_y, B + 1)
            nc.vector.tensor_tensor(h_res[0:B, CLS, :], ps[0:B, 2, 0:D], h_res[0:B, CLS, :], ALU.add).then_inc(s_ye, 1)
            dve.wait_ge(s_ye, B + 2)
            deviation_inputs(1, B - 1)
            normalise(1, B - 1)

            def over_experts(x):
                return x.rearrange("p (t a) -> p t a", a=1).to_broadcast([P, NT, NE])

            def less_maximum():
                dve.wait_ge(s_rl, NT)
                late = ps[:, 7, EARLY * NE:NT * NE].rearrange("p (t e) -> p t e", e=NE)
                link(nc.vector.tensor_copy(logit[:, EARLY:], late))
                link(nc.vector.tensor_reduce(row[:, 0], logit[:], AX_X, ALU.max))
                nc.vector.tensor_tensor(logit[:], logit[:], over_experts(row[:, 0]), ALU.subtract).then_inc(s_rm, 1)

            def scores():
                dve.wait_ge(s_re, 1)
                link(nc.vector.tensor_reduce(row[:, 1], score[:], AX_X, ALU.add))
                link(nc.vector.reciprocal(row[:, 2], row[:, 1]))
                link(nc.vector.tensor_tensor(score[:], score[:], over_experts(row[:, 2]), ALU.mult))

            def best_scores():
                for t in range(NT):
                    last = nc.vector.max(top[:, t], score[:, t])
                link(last)

            def best_experts():
                for t in range(NT):
                    last = nc.vector.max_index(top_at[:, t], top[:, t], score[:, t])
                link(last)
                link(nc.vector.tensor_copy(top_f[:], top_at[:]))

            def picks():
                experts_row = iota_sb[:, SLOT_TILES:].rearrange("p (a e) -> p a e", a=1).to_broadcast([P, NT, NE])
                for j in range(2):
                    link(nc.vector.tensor_tensor(pick[j][:], experts_row, top_f[:, :, j:j + 1].to_broadcast([P, NT, NE]), ALU.is_equal))
                    link(nc.vector.tensor_tensor(pick[j][:], pick[j][:], over_experts(valid_sb[:]), ALU.mult))
                nc.vector.tensor_tensor(mask[:], pick[0][:], pick[1][:], ALU.add).then_inc(s_mask, 1)
                link(nc.vector.tensor_tensor(row[:, 3], top[:, :, 0], top[:, :, 1], ALU.add))
                link(nc.vector.tensor_scalar(row[:, 3], row[:, 3], 1e-8, None, ALU.add))
                link(nc.vector.reciprocal(row[:, 0], row[:, 3]))
                for j in range(2):
                    last = nc.vector.tensor_tensor(weight[:, j], top[:, :, j], row[:, 0], ALU.mult)
                link(last)

            def places():
                dve.wait_ge(s_cnt, 1)
                in_tile = ps[:, 6, 0:NT * NE].rearrange("p (t e) -> p t e", e=NE)
                of_tile = ps[:, 6, NT * NE:2 * NT * NE].rearrange("p (t e) -> p t e", e=NE)
                link(nc.vector.tensor_copy(place[:], of_tile))
                for e in range(NE):
                    last = nc.vector.tensor_tensor_scan(total[:, :, e], ones[:, 0:NT], place[:, :, e], 0.0, ALU.mult, ALU.add)
                link(last)
                link(nc.vector.tensor_tensor(place[:], total[:], place[:], ALU.subtract))
                link(nc.vector.tensor_tensor(place[:], place[:], in_tile, ALU.add))
                link(nc.vector.tensor_scalar(tiles_i[:], total[:, CLS], 1.0 / P, 0.5 - 0.5 / P, ALU.mult, ALU.add))
                link(nc.vector.tensor_copy(tiles_f[:, 0], tiles_i[:]))
                link(nc.vector.tensor_tensor_scan(tiles_f[:, 1], ones[:, 0:NE], tiles_f[:, 0], 0.0, ALU.mult, ALU.add))
                link(nc.vector.tensor_tensor(tiles_f[:, 2], tiles_f[:, 1], tiles_f[:, 0], ALU.subtract))
                link(nc.vector.tensor_scalar(tiles_f[:, 2], tiles_f[:, 2], float(P), None, ALU.mult))

            def slots():
                link(nc.vector.tensor_tensor(place[:], place[:], tiles_f[:, 2:3].to_broadcast([P, NT, NE]), ALU.add))
                for j in range(2):
                    link(nc.vector.tensor_tensor(pick[j][:], pick[j][:], place[:], ALU.mult))
                    link(nc.vector.tensor_reduce(slot_f[:], pick[j][:], AX_X, ALU.add))
                    nc.vector.tensor_copy(slot[:, j], slot_f[:]).then_inc(s_slot, 1)
                    dve.wait_ge(s_slot, j + 1)
                link(nc.vector.tensor_tensor(before[:], tiles_f[0:1, 1:2].to_broadcast([1, SLOT_TILES, NE]),
                                             iota_sb[0:1, 0:SLOT_TILES].rearrange("p (t a) -> p t a", a=1).to_broadcast([1, SLOT_TILES, NE]), ALU.is_le))
                link(nc.vector.tensor_reduce(expert_f[:], before[:], AX_X, ALU.add))
                nc.vector.tensor_scalar(expert_i[:], expert_f[:], float(NE - 1), None, ALU.min).then_inc(s_te, 1)

            def low_part(p):
                dve.wait_ge(s_exhigh, p + 1)
                nc.vector.scalar_tensor_tensor(out=ex16[:, bass.ds(p * (2 * ROW) + ROW, ROW)], in0=raw_flat[:, bass.ds(p * ROW, ROW)],
                                               scalar=w_up[0:KH], in1=ex16[:, bass.ds(p * (2 * ROW), ROW)],
                                               op0=ALU.mult, op1=ALU.subtract).then_inc(s_exlow, 1)

            def hidden_chunk(u, c, hidden):
                dve.wait_ge(s_silu, u + 1)
                nc.vector.scalar_tensor_tensor(out=hidden[:, c % 2], in0=ps[:, 2 * (c % 2) + 1, :], scalar=gu_down[:],
                                               in1=hidden[:, c % 2], op0=ALU.mult, op1=ALU.mult).then_inc(s_h, 1)

            def hidden_class(u, hidden):
                dve.wait_ge(s_silu, u + 1)
                nc.vector.scalar_tensor_tensor(out=hidden[:, 0, 0:FC * B], in0=ps[:, 7, 0:FC * B], scalar=gu_down[:],
                                               in1=hidden[:, 0, 0:FC * B], op0=ALU.mult, op1=ALU.mult).then_inc(s_h, 1)

            def shared_out(s, b):
                dve.wait_ge(s_dn, unit(s, b, FC) + 2)
                for t in range(TPB):
                    h = h_res[:, bass.ds(b * TPB + t, 1), :]
                    last = nc.vector.scalar_tensor_tensor(out=h, in0=y_tile(t).rearrange("p (a d) -> p a d", a=1), scalar=1.0 / NS, in1=h,
                                                          op0=ALU.mult, op1=ALU.add)
                last.then_inc(s_ya, 1)

            def shared_out_class(s):
                dve.wait_ge(s_dn, unit(s, B, 0) + 3)
                nc.vector.scalar_tensor_tensor(out=h_res[0:B, CLS, :], in0=ps[0:B, 7, 0:D], scalar=1.0 / NS, in1=h_res[0:B, CLS, :],
                                               op0=ALU.mult, op1=ALU.add).then_inc(s_ya, 1)

            raw_flat = ex_raw[:].rearrange("p e k n -> p (e k n)")
            for c in range(FC):
                hidden_chunk(unit(0, 0, c), c, sh_h)
            less_maximum()
            for c in range(FC):
                if FIRST <= c < FIRST + PIECES:
                    low_part(c - FIRST)
                hidden_chunk(unit(0, 1, c), c, sh_h)
                if c == 0:
                    shared_out(0, 0)
                    scores()
                    best_scores()
                if c == 1:
                    best_experts()
                if c == 2:
                    picks()
                if c == 3:
                    places()
                if c == 4:
                    slots()
            with dve.Fori(2, B) as b:
                for c in range(FC):
                    low_part(PIECES + (b - 2) * FC + c)
                    hidden_chunk(unit(0, b, c), c, sh_h)
                    if c == 0:
                        shared_out(0, b - 1)

            dve.wait_ge(s_scat, 16 * 2 * NT)

            def slot_columns(j, n):
                dve.wait_ge(s_xt, j + 1)
                moved = ps[0:KH, 3 * n, 0:2 * P].rearrange("p (k n) -> p k n", k=2)
                nc.vector.tensor_scalar(sx_t[n][:, 0], moved, X_UP, None, ALU.mult).then_inc(s_xte, 1)
                dve.wait_ge(s_xte, 2 * j + 1)
                nc.vector.scalar_tensor_tensor(out=sx_t[n][:, 1], in0=moved, scalar=X_UP, in1=sx_t[n][:, 0],
                                               op0=ALU.mult, op1=ALU.subtract).then_inc(s_xte, 1)

            def routed_hidden(j, n):
                dve.wait_ge(s_rs, j + 1)
                up = ps[:, 3 * n:3 * n + 3, :].rearrange("p a n -> p (a n)")[:, FF:2 * FF]
                nc.vector.scalar_tensor_tensor(out=hid[:, n], in0=up, scalar=gu_down[:], in1=hid[:, n],
                                               op0=ALU.mult, op1=ALU.mult).then_inc(s_rh, 1)

            def routed_out(j, n):
                dve.wait_ge(s_ry, j + 1)
                nc.vector.tensor_copy(sy[:, n], ps[:, 7, 256:256 + D]).then_inc(s_rye, 1)

            slot_columns(0, 0)
            hidden_class(CLASS_UNIT, sh_h)
            shared_out(0, B - 1)
            shared_out_class(0)
            slot_columns(1, 1)
            routed_hidden(0, 0)
            for n in range(2):
                slot_columns(2 + n, n)
                routed_hidden(1 + n, 1 - n)
                routed_out(n, n)
            with dve.Fori(1, SLOT_TILES // 2 - 1) as i:
                for n in range(2):
                    slot_columns(2 * i + 2 + n, n)
                    routed_hidden(2 * i + 1 + n, 1 - n)
                    dve.wait_ge(s_rst[n], 16 * i)
                    routed_out(2 * i + n, n)
            routed_hidden(SLOT_TILES - 1, 1)
            for n in range(2):
                dve.wait_ge(s_rst[n], 16 * (SLOT_TILES // 2 - 1))
                routed_out(SLOT_TILES - 2 + n, n)

            def combine(b, own, j):
                if j == 0:
                    dve.wait_ge(s_gat[b], 16 * 2 * len(own))
                for t in own:
                    r = tile_rows(t)
                    last = nc.vector.scalar_tensor_tensor(out=h_res[0:r, t], in0=gat[0:r, j, t], scalar=weight[0:r, j, t:t + 1],
                                                          in1=h_res[0:r, t], op0=ALU.mult, op1=ALU.add)
                link(last)

            dve.wait_ge(s_ry, SLOT_TILES)
            for b in range(B):
                own = [b * TPB + t for t in range(TPB)]
                for c in range(FC):
                    hidden_chunk(unit(1, b, c), c, sh_h1)
                    if c == 0 and b > 0:
                        shared_out(1, b - 1)
                    if c in (2, 4):
                        combine(b, own, c // 2 - 1)
            combine(B, [CLS], 0)
            combine(B, [CLS], 1)
            hidden_class(unit(1, B, 0), sh_h1)
            shared_out(1, B - 1)
            shared_out_class(1)

        @block.tensor
        def _(pe):
            mm = nc.tensor.matmul
            def tokens(step, r, w, first, last, second=False):
                for which in range(2):
                    pe.wait_ge(s_feat, 2 * RING + 2 * step + which + 1)
                    for j in range(HT_):
                        if second and first and which == 0:
                            pe.wait_ge(s_hrow, j + 1)
                        ins = mm(ps[:, j, 0:D], feat[r][:, which, j * P:(j + 1) * P], w(which),
                                 start=first and which == 0, stop=last and which == 1)
                ins.then_inc(s_used, 1)

            flat = w_tok_sb[:].rearrange("p s a d -> p (s a d)")
            for half in range(2):
                if half == 0:
                    pe.wait_ge(s_wtok[0], 16)
                for k in range(BANDS):
                    if half == 0 and k == 1:
                        pe.wait_ge(s_wtok[1], 16)
                    tokens(half * STEPS + k, k % RING, lambda a: w_tok_sb[:, k, a], k == 0, False, half == 1)
                if half == 0:
                    pe.wait_ge(s_wtok[2], 16)
                with pe.Fori(1, XB) as c:
                    for k in range(BANDS):
                        tokens(half * STEPS + c * BANDS + k, k % RING,
                               lambda a: flat[:, bass.ds((c * BANDS + k) * 2 * D + a * D, D)], False, False)
                for k in range(BANDS // 2):
                    s = XB * BANDS + k
                    tokens(half * STEPS + s, k % RING, lambda a: w_tok_sb[:, s, a], False, k == BANDS // 2 - 1)

            def transposed_tokens(n, group, part=slice(None)):
                pe.wait_ge(s_xn, n * B + group + 1)
                for j, t in list(enumerate(tiles_of(group, n == 1)))[part]:
                    r, at_ = tile_rows(t), order(n, group) + j
                    if at_ >= transposed_at_once(n, group):
                        pe.wait_ge(s_xnt, n * NT + at_ - transposed_at_once(n, group) + 1)
                    for k in range(2):
                        ins = nc.tensor.transpose(ps[0:KH, bank(n, group, j), k * r:(k + 1) * r], xn[0:r, t, k * KH:(k + 1) * KH], ident[0:r, 0:r])
                    ins.then_inc(s_xnp, 1)

            def project(b, chunks):
                for c in chunks:
                    if c >= 2:
                        pe.wait_ge(s_qe, b * CH + c - 1)
                    for k in range(2):
                        ins = mm(ps[:, c % 2, :], w_qkv_sb[:, k, c * P:(c + 1) * P], xn_t[:, k, bass.ds(b * SEQ, SEQ)],
                                 start=k == 0, stop=k == 1)
                    ins.then_inc(s_q, 1)

            def project_class():
                for c in range(CH):
                    for k in range(2):
                        ins = mm(ps[:, 2, c * B:(c + 1) * B], w_qkv_sb[:, k, c * P:(c + 1) * P], xn_t[:, k, NX:T],
                                 start=k == 0, stop=k == 1)
                ins.then_inc(s_qcls, 1)

            def logits(b, again=True):
                pe.wait_ge(s_nl, b + 1)
                half_ = bass.ds(b % 2, 1)
                for c in range(CH):
                    mm(ps[0:NH, 3, :], norm_lhs[:, c], w_sq[:, half_, c], start=c == 0, stop=c == CH - 1)
                if again:
                    pe.wait_ge(s_wo, 2 * b - 1)
                for c in range(CH):
                    ins = mm(ps[0:NH, 2, 32:33], norm_lhs[:, c], w_cls_sq[:, bass.ds(b, 1), c:c + 1], start=c == 0, stop=c == CH - 1)
                ins.then_inc(s_lg, 1)

            def spread_pi(b, chunks=range(CH)):
                pe.wait_ge(s_pi, b + 1)
                for c in chunks:
                    if c >= 2:
                        pe.wait_ge(s_pbe, b * CH + c - 1)
                    mm(ps[:, 6 + c % 2, :], spread_r[:, c], pi_high[:], start=True, stop=False)
                    mm(ps[:, 6 + c % 2, :], spread_r[:, c], pi_low[:], start=False, stop=True).then_inc(s_pb, 1)
                    if c == CH - 1:
                        pe.wait_ge(s_pisum, b + 1)
                        for i in range(CH):
                            ins = mm(ps[:, 2, P + 2 * i:P + 2 * i + 2], spread_sb[:, i], pi[:, SEQ:SEQ + 2], start=True, stop=True)
                        ins.then_inc(s_pb, 1)

            def attention_out(b):
                pe.wait_ge(s_wo, 2 * b + 2)
                pe.wait_ge(s_ye, b + 1)
                for c in range(CH):
                    for t in range(TPB):
                        ins = mm(y_tile(t), wp[:, c, t * P:(t + 1) * P], w_out_b[:, c], start=c == 0 and t % 2 == 0, stop=c == CH - 1,
                                 skip_group_check=True)
                ins.then_inc(s_y, 1)

            pe.wait_ge(s_const, 16 * 5)
            pe.wait_ge(s_hrow, HT_ + HT_ - 4)
            transposed_tokens(0, 0)
            pe.wait_ge(s_hrow, 2 * HT_)
            pe.wait_ge(s_peak, 1)
            nc.tensor.transpose(ps[0:1, 3, 0:P], peak[:, 0:1], ident[:]).then_inc(s_peakt, 1)
            pe.wait_ge(s_attnw, 16 * 6)
            pe.wait_ge(s_xnt, TPB + 1)
            project_class()
            project(0, [0])
            pe.wait_ge(s_peak, 2)
            mm(ps[:, 3, P:P + 1], ones[0:1], peak[0:1, 1:2], start=True, stop=True).then_inc(s_peakt, 1)
            project(0, range(1, CH))
            transposed_tokens(0, 1)
            logits(0, False)
            transposed_tokens(0, 2)
            transposed_tokens(0, 3)
            pe.wait_ge(s_xnt, NT)
            with pe.Fori(0, B - 1) as b:
                pe.wait_ge(s_qe, (b + 1) * CH)
                for c in range(CH):
                    project(b + 1, [c])
                    spread_pi(b, [c])
                logits(b + 1)
                attention_out(b)

            def router_logits(tiles):
                for t in tiles:
                    r = tile_rows(t)
                    pe.wait_ge(s_xnt, NT + t + 1)
                    for k in range(2):
                        ins = mm(ps[0:r, 3 if t < EARLY else 7, t * NE:(t + 1) * NE], cols_sb[:, t % COLS, k, 0:r], gate_sb[:, k], start=k == 0, stop=k == 1)
                    ins.then_inc(s_rl, 1)

            pe.wait_ge(s_qe, B * CH)
            pe.wait_ge(s_mx, B)
            for c in range(CH):
                spread_pi(B - 1, [c])
                if c >= CH - TPB:
                    transposed_tokens(1, 0, slice(c - (CH - TPB), c - (CH - TPB) + 1))
            router_logits(range(TPB))
            attention_out(B - 1)
            for c in range(CH):
                ins = mm(ps[0:B, 2, 0:D], wp_cls[:, c], w_out_sb[:, c], start=c == 0, stop=c == CH - 1)
            ins.then_inc(s_y, 1)

            def gate_up_products(s, c, u, tok, out):
                piece, at_ = divmod(u * FF + c * P, PIECE)
                for k in range(2):
                    for w, x in ((0, 0), (0, 1), (1, 0)):
                        ins = mm(out, sh16[s][:, k * (GU_PIECES // 2) + piece, w, at_:at_ + P], x16[:, x, k, tok],
                                 start=k == w == x == 0, stop=k == w == 1)
                return ins

            def shared_gate(s, b, c, tok):
                if c >= 2:
                    pe.wait_ge(s_h, unit(s, b, c) - 1)
                gate_up_products(s, c, 0, tok, ps[:, 2 * (c % 2), :])

            def shared_up(s, b, c, tok):
                gate_up_products(s, c, 1, tok, ps[:, 2 * (c % 2) + 1, :]).then_inc(s_gu, 1)

            def shared_gate_up(s, b, c, tok):
                shared_gate(s, b, c, tok)
                shared_up(s, b, c, tok)

            def shared_down(s, b, c, hidden):
                pe.wait_ge(s_h, unit(s, b, c) + 1)
                if c == 0:
                    pe.wait_ge(s_ya, s * (B + 1) + b + 1)
                for t in range(TPB):
                    ins = mm(y_tile(t), hidden[:, c % 2, t * P:(t + 1) * P], sh_dn_sb[s][:, c], start=c == 0 and t % 2 == 0, stop=c == FC - 1,
                             skip_group_check=True)
                ins.then_inc(s_dn, 1)

            def shared_block(s, b, hidden):
                tok = bass.ds(b * SEQ, SEQ)
                shared_gate_up(s, b, 0, tok)
                shared_down(s, b - 1, FC - 1, hidden)
                for c in range(1, FC):
                    shared_gate_up(s, b, c, tok)
                    shared_down(s, b, c - 1, hidden)

            def shared_class(s):
                for u in range(2):
                    for c in range(FC):
                        ins = gate_up_products(s, c, u, slice(NX, T), ps[:, 6 + u, c * B:(c + 1) * B])
                ins.then_inc(s_gu, 1)

            def shared_class_down(s, hidden):
                pe.wait_ge(s_h, unit(s, B, 0) + 1)
                for c in range(FC):
                    ins = mm(ps[0:B, 7, 0:D], hidden[:, 0, c * B:(c + 1) * B], sh_dn_sb[s][:, c], start=c == 0, stop=c == FC - 1)
                ins.then_inc(s_dn, 1)

            def tile_between(c, place_):
                t = BETWEEN.get((c, place_))
                if t is not None:
                    group = min(t // TPB, B - 1)
                    transposed_tokens(1, group, slice(t - group * TPB, t - group * TPB + 1))
                    if t > TPB:
                        router_logits([t - 1])

            first = slice(0, SEQ)
            pe.wait_ge(s_split[0], 1)
            pe.wait_ge(s_xl, TPB)
            for c in range(FC):
                if c == 1:
                    pe.wait_ge(s_re1, 1)
                    pe.wait_ge(s_ye, B + 2)
                shared_gate(0, 0, c, first)
                tile_between(c, 0)
                shared_up(0, 0, c, first)
                tile_between(c, 1)
                if c > 0:
                    shared_down(0, 0, c - 1, sh_h)
                tile_between(c, 2)
            router_logits([CLS])
            pe.wait_ge(s_xl, NT)
            second = slice(SEQ, 2 * SEQ)
            shared_gate_up(0, 1, 0, second)
            shared_down(0, 0, FC - 1, sh_h)
            for c in range(1, FC):
                shared_gate_up(0, 1, c, second)
                shared_down(0, 1, c - 1, sh_h)
                if c == 3:
                    pe.wait_ge(s_mask, 1)
                    masks = mask[:].rearrange("p t e -> p (t e)")
                    mm(ps[:, 6, 0:NT * NE], tri[:], masks, start=True, stop=True)
                    mm(ps[:, 6, NT * NE:2 * NT * NE], ones[:], masks, start=True, stop=True).then_inc(s_cnt, 1)
            with pe.Fori(2, B) as b:
                shared_block(0, b, sh_h)
            shared_class(0)

            dn_flat = ex_dn_sb[:].rearrange("p e c d -> p (e c d)")

            def expert_of(j):
                return pe.value_load(expert_i[0:1, bass.ds(j, 1)], min_val=0, max_val=NE - 1)

            def slot_transposes(n, loads):
                pe.wait_ge(s_sxe[n], 16 * loads)
                for k in range(2):
                    ins = nc.tensor.transpose(ps[0:KH, 3 * n, k * P:(k + 1) * P], sx[:, n, k * KH:(k + 1) * KH], ident[:])
                ins.then_inc(s_xt, 1)

            def gate_up(n, e, parts):
                for q in parts:
                    for k in range(2):
                        for x, w in ((0, 0), (0, 1), (1, 0)):
                            at_ = (k * 2 + w) * ROW + q * 512
                            ins = mm(ps[:, 3 * n + q, :], sx_t[n][:, x, k], ex16[:, bass.ds(e * (2 * GU) + at_, 512)],
                                     start=k == w == x == 0, stop=k == x == 1)
                return ins

            def hidden_transposes(j, n):
                pe.wait_ge(s_rh, j + 1)
                pe.wait_ge(s_rye, j + 1)
                for c in range(FC):
                    ins = nc.tensor.transpose(ps[:, 6 + c // 4, (c % 4) * P:(c % 4 + 1) * P], hid[:, n, c * P:(c + 1) * P], ident[:])
                ins.then_inc(s_ht, 1)

            def down(j, n, e):
                pe.wait_ge(s_hte, j + 1)
                for c in range(FC):
                    ins = mm(ps[:, 7, 256:256 + D], hid_t[n][:, c], dn_flat[:, bass.ds(e * (FC * D) + c * D, D)], start=c == 0, stop=c == FC - 1)
                ins.then_inc(s_ry, 1)

            def routed(j, n, e, e_before, loads):
                pe.wait_ge(s_xte, 2 * j + 2)
                gate_up(n, e, [0])
                hidden_transposes(j - 1, 1 - n)
                gate_up(n, e, [1, 2]).then_inc(s_rg, 1)
                if loads is not None:
                    slot_transposes(1 - n, loads)
                down(j - 1, 1 - n, e_before)

            slot_transposes(0, 1)
            shared_down(0, B - 1, FC - 1, sh_h)
            shared_class_down(0, sh_h)
            pe.wait_ge(s_te, 1)
            pe.wait_ge(s_exd, 16 * NE)
            pe.wait_ge(s_exlow, 2 * NE)
            e = expert_of(0)
            pe.wait_ge(s_xte, 2)
            gate_up(0, e, [0, 1, 2]).then_inc(s_rg, 1)
            pe.wait_ge(s_ya, B + 2)
            slot_transposes(1, 1)
            with pe.Fori(0, SLOT_TILES // 2 - 1) as i:
                e = [expert_of(2 * i + n) for n in range(3)]
                for n in range(2):
                    routed(2 * i + 1 + n, 1 - n, e[n + 1], e[n], i + 2)
            last = SLOT_TILES - 1
            e = [expert_of(last - 1), expert_of(last)]
            routed(last, 1, e[1], e[0], None)
            pe.wait_ge(s_split[1], 3 * GU_PIECES)
            shared_gate_up(1, 0, 0, slice(0, SEQ))
            hidden_transposes(last, 1)
            down(last, 1, e[1])

            for c in range(1, FC):
                shared_gate_up(1, 0, c, slice(0, SEQ))
                shared_down(1, 0, c - 1, sh_h1)
            with pe.Fori(1, B) as b:
                shared_block(1, b, sh_h1)
            shared_class(1)
            shared_down(1, B - 1, FC - 1, sh_h1)
            shared_class_down(1, sh_h1)


def _layouts(i):
    f = i["L0_tok_freq_bands"]
    w = i["L0_tok_W"].reshape(D, VALS, 2, BANDS).transpose(1, 3, 2, 0)
    full = w[:XB * P].reshape(XB, P, BANDS, 2, D).transpose(1, 0, 2, 3, 4).reshape(P, XB * BANDS, 2, D)
    left = w[XB * P:].reshape(LEFT, BANDS // 2, 2, 2, D).transpose(2, 0, 1, 3, 4).reshape(P, BANDS // 2, 2, D)

    def gate_up(g, u):
        both = np.concatenate([g, u], axis=1)
        return both.transpose(0, 2, 1).reshape(len(g), 2, KH, 2 * FF).transpose(0, 2, 1, 3)

    def down(d):
        return d.transpose(0, 2, 1).reshape(len(d), FC, P, D).transpose(0, 2, 1, 3)

    channel = np.arange(INNER)
    heads = (channel[:, None] // DH == np.arange(NH)).astype(np.float32)
    return {
        "x_t": i["x"].reshape(NX, VALS).T,
        "freqs": np.concatenate([np.tile(f, (P, 1)), np.repeat(f.reshape(BANDS // 2, 2), LEFT, axis=1).T], axis=1),
        "w_tok": np.concatenate([full, left], axis=1),
        "cls4": np.tile(i["cls_tok"].reshape(1, D), (B, 1)),
        "w_qkv": i["L0_attn_w_qkv"].reshape(2, KH, INNER).transpose(1, 0, 2),
        "temp": i["L0_attn_temp"],
        "w_out": i["L0_attn_w_out"].reshape(CH, P, D).transpose(1, 0, 2),
        "b_out": np.tile(i["L0_attn_b_out"], (P, 1)),
        "gate_t": i["L0_ffn_gate_w"].T.reshape(2, KH, NE).transpose(1, 0, 2),
        "gu": np.concatenate([gate_up(i["L0_ffn_shared_gate"], i["L0_ffn_shared_up"]),
                              gate_up(i["L0_ffn_routed_gate"], i["L0_ffn_routed_up"])]),
        "sh_dn": down(i["L0_ffn_shared_down"]),
        "ex_dn": down(i["L0_ffn_routed_down"]),
        "c_ident": np.eye(P, dtype=np.float32),
        "c_tri": np.triu(np.ones((P, P), np.float32), 1),
        "c_heads": heads.reshape(CH, P, NH).transpose(1, 0, 2),
        "c_spread": heads.T.reshape(NH, CH, P),
        "c_iota": np.tile(np.concatenate([np.arange(SLOT_TILES), np.arange(NE)]).astype(np.float32), (P, 1)),
        "c_valid": (np.arange(P)[:, None] < np.where(np.arange(NT) < CLS, P, B)).astype(np.float32),
    }


def kernel(**inputs):
    import concourse.bacc as bacc
    from concourse.bass_utils import run_bass_kernel_spmd

    nc = bacc.Bacc("TRN2", target_bir_lowering=False, num_devices=1)
    arrays = {k: np.ascontiguousarray(v) for k, v in _layouts({k: np.asarray(v) for k, v in inputs.items()}).items()}
    args = {k: nc.dram_tensor(k, v.shape, F32, kind="ExternalInput").ap() for k, v in arrays.items()}
    args["out"] = nc.dram_tensor("out", (B, SEQ + 1, D), F32, kind="ExternalOutput").ap()
    args["slots_x"] = nc.dram_tensor("slots_x", (SLOTS, D), F32).ap()
    args["slots_y"] = nc.dram_tensor("slots_y", (SLOTS, D), F32).ap()
    vit_tower(nc, **args)
    result = run_bass_kernel_spmd(nc, [arrays], core_ids=[0])
    return result.results[0]["out"]
```
